# Optimizing a Trainium2 kernel written in Bass

```python
import numpy as np
import jax
import jax.numpy as jnp

def _softmax(x, axis=-1):
    return jax.nn.softmax(x, axis=axis)

def _gelu(x):
    return jax.nn.gelu(x, approximate=True)

def _silu(x):
    return jax.nn.silu(x)

def _sigmoid(x):
    return jax.nn.sigmoid(x)

def _layernorm(x, axis=-1, eps=1e-05):
    m = jnp.mean(x, axis=axis, keepdims=True)
    v = jnp.var(x, axis=axis, keepdims=True)
    return (x - m) / jnp.sqrt(v + eps)

def _scatter_add(tgt, idx, src, axis=0):
    return tgt.at[idx].add(src)

def _segment_sum(src, seg, n):
    return jax.ops.segment_sum(src, seg, n)
kernel_name = 'mk_flamingo_gated_d1_seqx_r8_5731e6'

def setup_inputs(seed: int=0):
    np.random.seed(seed)
    _w = jnp.asarray

    def _rec_inputs():
        import jax
        import jax.numpy as jnp
        _rk = jax.random.key(seed)
        x = -0.000125 + 0.9999 * jax.random.normal(jax.random.fold_in(_rk, 1), (8, 256, 256), jnp.float32)
        _lenS = 256 - jax.random.randint(jax.random.fold_in(_rk, 7), (8,), 0, max(1, 256 // 4) + 1, jnp.int32)
        _lenS2 = 64 - jax.random.randint(jax.random.fold_in(_rk, 8), (8,), 0, max(1, 64 // 4) + 1, jnp.int32)
        _ctx_2048P = jax.random.normal(jax.random.fold_in(_rk, 11), (8, 16, 256), jnp.float32)
        _ctx_2048c = jax.random.dirichlet(jax.random.fold_in(_rk, 511), 0.3 * jnp.ones((16,), jnp.float32), (8, 64))
        _ctx_2048t = jnp.einsum('bsk,bkd->bsd', _ctx_2048c, _ctx_2048P)
        _ctx_2048t = _ctx_2048t * jax.lax.rsqrt(jnp.mean(jnp.square(_ctx_2048t)) + 1e-12) * 0.953939
        ctx_2048 = 0.00222621 + 0.99962 * (_ctx_2048t + 0.3 * jax.random.normal(jax.random.fold_in(_rk, 611), (8, 64, 256), jnp.float32))
        itok_Sx4_0_63 = jax.random.randint(jax.random.fold_in(_rk, 12), (256, 4), 0, 64, jnp.int32)
        _g = jax.random.normal(jax.random.fold_in(_rk, 9001), (2, 1), jnp.float32)
        _g = jnp.sign(_g) * jnp.maximum(jnp.abs(_g), 1.0) + (_g == 0) * 1.0
        g_xattn = _g[0]
        g_ffn = _g[1]
        return (x, ctx_2048, itok_Sx4_0_63, g_xattn, g_ffn)
    x, ctx_2048, itok_Sx4_0_63, g_xattn, g_ffn = _rec_inputs()

    def _L0_xattn_setup():
        import math
        import jax, jax.numpy as jnp
        import numpy as np
        B, S, D, N, K, TOPK = (4, 512, 256, 64, 4, 2)
        key = jax.random.key(seed)
        k0, k1, k2, k3, k4 = jax.random.split(key, 5)
        token_states = jax.random.normal(k0, (B, S, D), dtype=jnp.float32)
        set_states = jax.random.normal(k1, (B, N, D), dtype=jnp.float32)
        desc_router = jax.random.normal(k2, (N, D), dtype=jnp.float32)
        token_to_sets = jax.random.randint(k3, (S, K), 0, N)
        bound = 1.0 / math.sqrt(D)
        W_q = jax.random.uniform(k4, (D, D), jnp.float32, -bound, bound)
        b_q = jnp.zeros((D,), jnp.float32)
        return {'token_states': token_states, 'set_states': set_states, 'desc_router': desc_router, 'W_q': W_q, 'b_q': b_q, 'token_to_sets': token_to_sets}
    _L0_xattn_all = _L0_xattn_setup()
    _L0_xattn_in = {k: v for k, v in _L0_xattn_all.items() if k in ('desc_router', 'W_q', 'b_q')}
    del _L0_xattn_all

    def _L0_ffn_setup():
        import jax, jax.numpy as jnp
        import numpy as np
        from functools import partial
        E = 8
        K = 2
        H = 256
        F = 1024

        def _moe_forward(x, gate_w, gate_b, fc1_w, fc1_b, fc2_w, fc2_b, alpha):
            B_, S_, H_ = x.shape
            xf = x.reshape(-1, H_)
            logits = xf @ gate_w + gate_b
            top_val, top_idx = jax.lax.top_k(logits, K)
            gate_score = jax.nn.softmax(top_val, axis=-1)
            onehot = jax.nn.one_hot(top_idx, E, dtype=xf.dtype)
            comb = jnp.einsum('tk,tke->et', gate_score, onehot) * alpha[:, None]

            def body(acc, p):
                w1, b1, w2, b2, w = p
                h = jax.nn.gelu(xf @ w1 + b1, approximate=False)
                y = h @ w2 + b2
                return (acc + y * w[:, None], None)
            out0 = jnp.zeros_like(xf)
            out, _ = jax.lax.scan(body, out0, (fc1_w, fc1_b, fc2_w, fc2_b, comb))
            return out.reshape(B_, S_, H_)
        key = jax.random.key(seed)
        ks = jax.random.split(key, 8)
        s = 0.02
        return {'hidden_states': jax.random.normal(ks[0], (2, 256, H), jnp.float32), 'gate_w': jax.random.normal(ks[1], (H, E), jnp.float32) * s, 'gate_b': jax.random.normal(ks[2], (E,), jnp.float32) * s, 'fc1_w': jax.random.normal(ks[3], (E, H, F), jnp.float32) * s, 'fc1_b': jax.random.normal(ks[4], (E, F), jnp.float32) * s, 'fc2_w': jax.random.normal(ks[5], (E, F, H), jnp.float32) * s, 'fc2_b': jax.random.normal(ks[6], (E, H), jnp.float32) * s, 'alpha': jax.random.normal(ks[7], (E,), jnp.float32)}
    _L0_ffn_all = _L0_ffn_setup()
    _L0_ffn_in = {k: v for k, v in _L0_ffn_all.items() if k in ('gate_w', 'gate_b', 'fc1_w', 'fc1_b', 'fc2_w', 'fc2_b', 'alpha')}
    del _L0_ffn_all
    return {'x': x, 'ctx_2048': ctx_2048, 'itok_Sx4_0_63': itok_Sx4_0_63, 'g_xattn': g_xattn, 'g_ffn': g_ffn, 'L0_xattn_desc_router': _L0_xattn_in['desc_router'], 'L0_xattn_W_q': _L0_xattn_in['W_q'], 'L0_xattn_b_q': _L0_xattn_in['b_q'], 'L0_ffn_gate_w': _L0_ffn_in['gate_w'], 'L0_ffn_gate_b': _L0_ffn_in['gate_b'], 'L0_ffn_fc1_w': _L0_ffn_in['fc1_w'], 'L0_ffn_fc1_b': _L0_ffn_in['fc1_b'], 'L0_ffn_fc2_w': _L0_ffn_in['fc2_w'], 'L0_ffn_fc2_b': _L0_ffn_in['fc2_b'], 'L0_ffn_alpha': _L0_ffn_in['alpha']}

def reference(x, ctx_2048, itok_Sx4_0_63, g_xattn, g_ffn, L0_xattn_desc_router, L0_xattn_W_q, L0_xattn_b_q, L0_ffn_gate_w, L0_ffn_gate_b, L0_ffn_fc1_w, L0_ffn_fc1_b, L0_ffn_fc2_w, L0_ffn_fc2_b, L0_ffn_alpha):
    import jax
    import jax.numpy as jnp

    def _L0_xattn_ref(token_states, set_states, desc_router, W_q, b_q, token_to_sets):
        import math
        import jax, jax.numpy as jnp
        import numpy as np
        B, S, D, N, K, TOPK = (4, 512, 256, 64, 4, 2)
        batch, seq_len, d = token_states.shape
        num_sets = set_states.shape[1]
        scale = 1.0 / math.sqrt(d)
        q = jnp.einsum('bsd,ed->bse', token_states, W_q) + b_q
        scores = jnp.einsum('bse,ne->bsn', q, desc_router) * scale
        valid = token_to_sets >= 0
        mask = ((token_to_sets[:, :, None] == jnp.arange(num_sets)[None, None, :]) & valid[:, :, None]).any(axis=1)
        neg_inf = jnp.array(-jnp.inf, scores.dtype)
        scores = jnp.where(mask[None, :, :], scores, neg_inf)
        topk_vals, topk_idx = jax.lax.top_k(scores, TOPK)
        b_i = jnp.arange(batch)[:, None, None]
        s_i = jnp.arange(seq_len)[None, :, None]
        scores = jnp.full_like(scores, neg_inf).at[b_i, s_i, topk_idx].set(topk_vals)
        weights = jax.nn.softmax(scores, axis=-1)
        return jnp.einsum('bsn,bnd->bsd', weights, set_states)

    def _L0_ffn_ref(hidden_states, gate_w, gate_b, fc1_w, fc1_b, fc2_w, fc2_b, alpha):
        import jax, jax.numpy as jnp
        import numpy as np
        from functools import partial
        E = 8
        K = 2
        H = 256
        F = 1024

        def _moe_forward(x, gate_w, gate_b, fc1_w, fc1_b, fc2_w, fc2_b, alpha):
            B_, S_, H_ = x.shape
            xf = x.reshape(-1, H_)
            logits = xf @ gate_w + gate_b
            top_val, top_idx = jax.lax.top_k(logits, K)
            gate_score = jax.nn.softmax(top_val, axis=-1)
            onehot = jax.nn.one_hot(top_idx, E, dtype=xf.dtype)
            comb = jnp.einsum('tk,tke->et', gate_score, onehot) * alpha[:, None]

            def body(acc, p):
                w1, b1, w2, b2, w = p
                h = jax.nn.gelu(xf @ w1 + b1, approximate=False)
                y = h @ w2 + b2
                return (acc + y * w[:, None], None)
            out0 = jnp.zeros_like(xf)
            out, _ = jax.lax.scan(body, out0, (fc1_w, fc1_b, fc2_w, fc2_b, comb))
            return out.reshape(B_, S_, H_)
        return _moe_forward(hidden_states, gate_w, gate_b, fc1_w, fc1_b, fc2_w, fc2_b, alpha)
    x = x + jnp.tanh(g_xattn[0]) * _L0_xattn_ref(_layernorm(x, axis=-1), ctx_2048, L0_xattn_desc_router, L0_xattn_W_q, L0_xattn_b_q, itok_Sx4_0_63)
    x = x + jnp.tanh(g_ffn[0]) * _L0_ffn_ref(_layernorm(x, axis=-1), L0_ffn_gate_w, L0_ffn_gate_b, L0_ffn_fc1_w, L0_ffn_fc1_b, L0_ffn_fc2_w, L0_ffn_fc2_b, L0_ffn_alpha)
    return x

_drawn_inputs = setup_inputs


def setup_inputs(seed=0):
    import zlib

    import numpy as np

    out = dict(_drawn_inputs(seed))
    spreads = {'L0_xattn_b_q': (0.0, 0.1)}
    factors = {'L0_ffn_gate_b': 4.401, 'L0_ffn_fc1_b': 8.0, 'L0_ffn_fc2_b': 4.759}
    for name, (base, spread) in spreads.items():
        noise = np.random.default_rng([zlib.crc32(name.encode()), seed]).standard_normal(out[name].shape)
        drawn = base * np.exp(spread * noise) if base else spread * noise
        out[name] = jnp.asarray(drawn.astype(out[name].dtype))
    for name, factor in factors.items():
        out[name] = (out[name] * factor).astype(out[name].dtype)
    return out
```

```python
from contextlib import ExitStack

import concourse.bass as bass
from concourse import mybir

ALU = mybir.AluOpType
ACT = mybir.ActivationFunctionType
AX = mybir.AxisListType
F32 = mybir.dt.float32
F16 = mybir.dt.float16
I32 = mybir.dt.int32
U32 = mybir.dt.uint32

P = 128
X_SCALE = 16.0
W_SCALE = 128.0
H_SCALE = 16.0
MASKED = -1.0e30
NOWHERE = 1 << 24
EPS = 1e-5


class Count:

    def __init__(self):
        self.n = 0

    def up(self, by=1):
        self.n += by
        return self.n


def flamingo_block(nc, x, ctx_sets, token_sets, g_xattn, g_ffn, desc, w_q, b_q, gate_w, gate_b,
                   fc1_w, fc1_b, fc2_w, fc2_b, alpha, out):
    B, S, D = x.shape
    NS = ctx_sets.shape[1]
    KSET = token_sets.shape[1]
    E, _, F = fc1_w.shape
    T = B * S
    NT = T // P
    GT = 4
    NG = NT // GT
    KC = D // P
    FC = F // P
    HALVES = S // P
    CAP = T
    TILES = (2 * T - E) // P + E
    SPARE = TILES - 2 * T // P
    W_COMB = D
    W_TOK = W_COMB + E
    ROW = W_TOK + 1
    NU = 2 * E
    NSTAGE = 2
    assert KC == 2 and HALVES == 2 and D == 256 and NG == 4 and FC == 8 and TILES == 39

    xt = x.rearrange("b (h p) d -> p (b h) d", p=P)
    out_t = out[0:T, :].rearrange("(t p) d -> p t d", p=P)
    xsort = nc.dram_tensor("xsort", [E * CAP + SPARE * P, ROW], I32, kind="Internal").ap()

    with ExitStack() as stack:
        def sb(name, shape, dt=F32):
            return stack.enter_context(nc.sbuf_tensor(name, shape, dt))

        def sem(name):
            return stack.enter_context(nc.semaphore(name))

        w1hi = sb("w1hi", [P, E, KC, F], F16)
        w1lo = sb("w1lo", [P, E, KC, F], F16)
        w2hi = sb("w2hi", [P, E, FC, D], F16)
        w2lo = sb("w2lo", [P, E, FC, D], F16)
        wstage = sb("wstage", [P, NSTAGE, KC * F])
        arena = sb("arena", [P, NT, D])
        xs = arena
        xn = sb("xn", [P, GT, D])
        xnT = sb("xnT", [P, 2, 2, KC, P])
        rows = sb("rows", [P, 2, GT, ROW], I32)
        early = rows[:, :, :, :].rearrange("p g t w -> p (g t w)").bitcast(F32)
        wq_sb = early[:, 0:2 * D].rearrange("p (c d) -> p c d", c=KC)
        bq_bc = early[:, 2 * D:3 * D].rearrange("p (c q) -> p c q", c=KC)
        desc_sb = early[0:NS, 3 * D:4 * D]
        bias_rows = early[0:E * FC + KC, 4 * D:4 * D + P]
        ctx_buf = sb("ctx_buf", [P, B, D])
        ctx_sb = ctx_buf[0:NS, :, :]
        descT = sb("descT", [P, KC, NS])
        proj = sb("proj", [P, KC, NS])
        itok = sb("itok", [P, HALVES, KSET], I32)
        itok_f = sb("itok_f", [P, HALVES, KSET])
        maskbias = sb("maskbias", [P, HALVES, NS])
        gcol = sb("gcol", [P, 2])
        tg = sb("tg", [P, 2])
        gw_sb = sb("gw_sb", [P, KC, E])
        gb_bc = sb("gb_bc", [P, E])
        alpha_bc = sb("alpha_bc", [P, E])
        b2_sb = sb("b2_sb", [E, D])
        bias_cols = sb("bias_cols", [P, E * FC + KC])
        b1T = bias_cols[:, 0:E * FC].rearrange("p (e f) -> p e f", e=E)
        bq_col = bias_cols[:, E * FC:E * FC + KC]
        ident = sb("ident", [P, P])
        ident16 = sb("ident16", [P, P], F16)
        ones = sb("ones", [P, P])
        before = sb("before", [P, P])
        iota_i = sb("iota_i", [P, NS], I32)
        iota64 = sb("iota64", [P, NS])
        iota_ti = sb("iota_ti", [1, TILES], I32)
        iota_t = sb("iota_t", [1, TILES])
        region = sb("region", [P, E])
        part_i = sb("part_i", [P, 1], I32)
        part_f = sb("part_f", [P, 1])
        pad_row = sb("pad_row", [P, ROW], I32)
        stats = sb("stats", [P, NT, 6])
        neg_half = sb("neg_half", [P, GT])
        mv1 = sb("mv1", [P, NT, 2])
        rstd1 = sb("rstd1", [P, NT])
        shift1 = sb("shift1", [P, NT])
        mv2 = sb("mv2", [P, NT, 2])
        rstd2 = sb("rstd2", [P, NT])
        shift2 = sb("shift2", [P, NT])
        masked = sb("masked", [P, GT, NS])
        top8 = sb("top8", [P, 2, GT, 8])
        top8i = sb("top8i", [P, 2, GT, 8], U32)
        top2f = sb("top2f", [P, GT, 2])
        diff = sb("diff", [P, 2, GT])
        ediff = sb("ediff", [P, 2, GT])
        den = sb("den", [P, GT])
        wpair = sb("wpair", [P, GT, 2])
        wset = sb("wset", [P, 2, GT, NS])
        wsum = sb("wsum", [P, GT, NS])
        wT = sb("wT", [NS, GT, P])
        logit = sb("logit", [P, GT, E])
        gtop = sb("gtop", [P, 2, GT, 8])
        gtopi = sb("gtopi", [P, 2, GT, 8], U32)
        gtop2f = sb("gtop2f", [P, GT, 2])
        gdiff = sb("gdiff", [P, 2, GT])
        gediff = sb("gediff", [P, 2, GT])
        gden = sb("gden", [P, GT])
        gpair = sb("gpair", [P, GT, 2])
        onehot = sb("onehot", [P, GT, 2, E])
        oh_tmp = sb("oh_tmp", [P, GT, 2, E])
        alpha2 = sb("alpha2", [P, GT, 2])
        comb = sb("comb", [P, 2, GT, E])
        combT = sb("combT", [E, GT, P])
        picks = sb("picks", [P, NT, E])
        earlier = sb("earlier", [P, NT + 1, E])
        rank = sb("rank", [P, GT, E])
        slot_f = sb("slot_f", [P, GT, 2])
        slot_i = sb("slot_i", [P, NG, GT, 2], U32)
        cnt = sb("cnt", [P, E])
        cnt_i = sb("cnt_i", [P, E], I32)
        tl_i = sb("tl_i", [P, E], I32)
        tl = sb("tl", [P, E])
        ctl = sb("ctl", [P, E])
        pad_f = sb("pad_f", [P, E])
        pad_ok = sb("pad_ok", [P, E])
        pad_i = sb("pad_i", [P, E], U32)
        over = wset[0:1, :, :, :].rearrange("a k t n -> a (k t n)")[:, 0:TILES * E].rearrange("a (i e) -> a i e", e=E)
        over2 = wT[0:1, :, :].rearrange("a t p -> a (t p)")[:, 0:TILES * E].rearrange("a (i e) -> a i e", e=E)
        te_f = sb("te_f", [1, TILES])
        tc_f = sb("tc_f", [1, TILES])
        tr_f = sb("tr_f", [1, TILES])
        te_i = sb("te_i", [1, TILES], I32)
        tr_i = sb("tr_i", [1, TILES], I32)
        NX = 4
        xg = ctx_buf[:, :, :].rearrange("p b d -> p (b d)")[:, 0:NX * ROW].bitcast(I32).rearrange(
            "p (s w) -> p s w", s=NX)
        b1cur = sb("b1cur", [P, NX, FC])
        wcur = sb("wcur", [P, NX])
        tokcur = sb("tokcur", [P, NX], U32)
        xT = xnT[:, 0, :, :, :].rearrange("p t k q -> p (t k q)").bitcast(F16).rearrange(
            "p (s a k q) -> p s a k q", s=2, a=2, k=KC)
        y_sb = xn[:, 0:2, :]
        flat = arena[:, :, :].rearrange("p t d -> p (t d)")
        h32 = [flat[:, j * F:(j + 1) * F] for j in range(2)]
        hhi = [flat[:, 2 * F + j * F // 2:2 * F + (j + 1) * F // 2].bitcast(F16) for j in range(2)]
        hlo = [flat[:, 3 * F + j * F // 2:3 * F + (j + 1) * F // 2].bitcast(F16) for j in range(2)]

        bank = [stack.enter_context(nc.psum_tensor(f"bank{i}", [P, 512], F32)) for i in range(8)]

        x_in = [sem(f"x_in{g}") for g in range(NG)]
        small_in = sem("small_in")
        ctx_in = sem("ctx_in")
        w_in = [sem(f"w_in{s}") for s in range(NSTAGE)]
        w_hi = sem("w_hi")
        w_lo = sem("w_lo")
        pool_const = sem("pool_const")
        pool_step = sem("pool_step")
        vec_const = sem("vec_const")
        vec_step = sem("vec_step")
        gates_ready = sem("gates_ready")
        descT_ps = sem("descT_ps")
        descT_sb = sem("descT_sb")
        proj_ps = sem("proj_ps")
        proj_ready = sem("proj_ready")
        stats1 = sem("stats1")
        stats2 = sem("stats2")
        ln1 = sem("ln1")
        xn1_done = sem("xn1_done")
        tr1_ps = sem("tr1_ps")
        tr1_sb = sem("tr1_sb")
        tr_pairs = sem("tr_pairs")
        scores_ps = sem("scores_ps")
        scores_read = sem("scores_read")
        diff_ready = sem("diff_ready")
        exp_ready = sem("exp_ready")
        wset_ready = sem("wset_ready")
        wT_ps = sem("wT_ps")
        wT_sb = sem("wT_sb")
        attn_ps = sem("attn_ps")
        x1_ready = sem("x1_ready")
        ln2 = sem("ln2")
        xn2_done = sem("xn2_done")
        tr2_ps = sem("tr2_ps")
        logits_ps = sem("logits_ps")
        hi_ready = sem("hi_ready")
        row_ready = sem("row_ready")
        logits_read = sem("logits_read")
        gdiff_ready = sem("gdiff_ready")
        gexp_ready = sem("gexp_ready")
        comb_ready = sem("comb_ready")
        picks_ready = sem("picks_ready")
        rank_ps = sem("rank_ps")
        rank_read = sem("rank_read")
        slots_ready = sem("slots_ready")
        combT_ps = sem("combT_ps")
        combT_sb = sem("combT_sb")
        b2_ps = sem("b2_ps")
        init_ready = sem("init_ready")
        out_init = sem("out_init")
        pad_out_init = sem("pad_out_init")
        scattered = [sem(f"scattered{r}") for r in range(2)]
        count_ps = sem("count_ps")
        pads_ready = sem("pads_ready")
        pads_out = sem("pads_out")
        table_ready = sem("table_ready")
        sorted_done = sem("sorted_done")
        b1T_ps = sem("b1T_ps")
        b1T_sb = sem("b1T_sb")
        xg_in = [sem(f"xg_in{s}") for s in range(NX)]
        b1_ready = sem("b1_ready")
        cur_ready = sem("cur_ready")
        xT_ps = sem("xT_ps")
        xT_sb = sem("xT_sb")
        fc1_ps = sem("fc1_ps")
        gelu_done = sem("gelu_done")
        hi_done = sem("hi_done")
        lo_done = sem("lo_done")
        y_ps = sem("y_ps")
        y_ready = sem("y_ready")
        add_started = sem("add_started")
        added = sem("added")

        NSMALL = 11

        def unit_parts(u):
            e = u // 2
            if u % 2 == 0:
                return w1hi[:, e].rearrange("p k f -> p (k f)"), w1lo[:, e].rearrange("p k f -> p (k f)")
            return w2hi[:, e].rearrange("p k f -> p (k f)"), w2lo[:, e].rearrange("p k f -> p (k f)")

        UNITS = [1, 1, 2, 2, 2, 2]
        unit_at = [sum(UNITS[:s]) for s in range(len(UNITS) + 1)]
        STEPS = NG + 2

        block = stack.enter_context(nc.Block())

        @block.sync
        def _(sp):
            def load_unit(u):
                e, s = u // 2, u % NSTAGE
                if u >= NSTAGE:
                    sp.wait_ge(w_hi, u - NSTAGE + 1)
                    sp.wait_ge(w_lo, u - NSTAGE + 1)
                if u % 2 == 0:
                    src = fc1_w[e].rearrange("(k p) f -> p k f", p=P)
                    dst = wstage[:, s, :].rearrange("p (k f) -> p k f", k=KC)
                else:
                    src = fc2_w[e].rearrange("(k p) d -> p k d", p=P)
                    dst = wstage[:, s, :].rearrange("p (k d) -> p k d", k=FC)
                sp.dma_start(dst, src).then_inc(w_in[s], 16)

            for g in range(NG):
                sp.dma_start(xs[:, g * GT:(g + 1) * GT, :], xt[:, g * GT:(g + 1) * GT, :]).then_inc(x_in[g], 16)
            for u in range(NU):
                load_unit(u)

            def load_tile(i, s):
                row = sp.value_load(tr_i[0:1, bass.ds(i, 1)], min_val=0, max_val=E * CAP + (SPARE - 1) * P)
                sp.dma_start(xg[:, s, :], xsort[bass.ds(row, P), :]).then_inc(xg_in[s], 16)

            sp.wait_ge(table_ready, 1)
            sp.wait_ge(sorted_done, 1)
            for i in range(NX):
                load_tile(i, i)
            with sp.Fori(1, TILES // NX) as m:
                for s in range(NX):
                    sp.wait_ge(cur_ready, m * NX + (s + 1 - NX))
                    load_tile(m * NX + s, s)
            for i in range(TILES // NX * NX, TILES):
                sp.wait_ge(cur_ready, i - NX + 1)
                load_tile(i, i % NX)

        @block.tensor
        def _(pe):
            pe.wait_ge(small_in, 16 * NSMALL)
            pe.wait_ge(pool_const, 1)
            for c in range(KC):
                mm = pe.transpose(bank[2][:, c * NS:(c + 1) * NS], desc_sb[:, c * P:(c + 1) * P], ident[0:NS, 0:NS])
            mm.then_inc(descT_ps, 1)
            nb = E * FC + KC
            pe.transpose(bank[4][:, 0:nb], bias_rows[:, :], ident[0:nb, 0:nb]).then_inc(b1T_ps, 1)
            pe.wait_ge(descT_sb, 1)
            for k in range(KC):
                for c in range(KC):
                    pe.matmul(bank[3][:, k * NS:(k + 1) * NS], wq_sb[:, c, k * P:(k + 1) * P], descT[:, c, :],
                              start=(c == 0), stop=(c == KC - 1))
            for c in range(KC):
                mm = pe.matmul(bank[3][:, 2 * NS:3 * NS], bq_bc[:, c, :], descT[:, c, :],
                               start=(c == 0), stop=(c == KC - 1))
            mm.then_inc(proj_ps, 1)

            pairs = Count()

            def transposed_pairs(g, done_sem, ps_sem, rhs, n, put):
                def products(j):
                    pe.wait_ge(tr_pairs, base + j + 1)
                    for t in range(2):
                        q = 2 * j + t
                        for k in range(KC):
                            mm = pe.matmul(put[:, q * n:(q + 1) * n], xnT[:, (base + j) % 2, t, k, :], rhs[:, k, :],
                                           start=(k == 0), stop=(k == KC - 1))
                    return mm
                base = pairs.n
                for j in range(2):
                    pe.wait_ge(done_sem, g * GT + 2 * j + 2)
                    if base + j >= 2:
                        pe.wait_ge(tr_pairs, base + j - 1)
                    for t in range(2):
                        for k in range(KC):
                            mm = pe.transpose(bank[(base + j) % 2][:, (t * KC + k) * P:(t * KC + k + 1) * P],
                                              xn[:, 2 * j + t, k * P:(k + 1) * P], ident[:, :])
                    mm.then_inc(ps_sem, 1)
                products(0)
                mm = products(1)
                pairs.up(2)
                return mm

            def scores(g):
                if g == 0:
                    pe.wait_ge(proj_ready, 1)
                if g >= 2:
                    pe.wait_ge(scores_read, g - 1)
                transposed_pairs(g, xn1_done, tr1_ps, proj, NS, bank[2 + g % 2]).then_inc(scores_ps, 1)

            def attention(g):
                pe.wait_ge(wset_ready, g + 1)
                if g == 0:
                    pe.wait_ge(b1T_sb, 1)
                if g >= 2:
                    pe.wait_ge(combT_sb, g - 1)
                for t in range(GT):
                    mm = pe.transpose(bank[4][0:NS, t * P:(t + 1) * P], wsum[:, t, :], ident[:, :])
                mm.then_inc(wT_ps, 1)
                pe.wait_ge(wT_sb, g + 1)
                if g == 0:
                    pe.wait_ge(ctx_in, 16)
                for j in range(2):
                    if g == 1:
                        pe.wait_ge(x1_ready, j + 1)
                    if g >= 2:
                        pe.wait_ge(init_ready, 2 * (g - 2) + j + 1)
                    for t in range(2):
                        q = 2 * j + t
                        mm = pe.matmul(bank[5 + j][:, t * D:(t + 1) * D], wT[:, q, :],
                                       ctx_sb[:, (g * GT + q) // HALVES, :], start=True, stop=True)
                    mm.then_inc(attn_ps, 1)

            def logits(g):
                if g >= 1:
                    pe.wait_ge(rank_read, g)
                transposed_pairs(g, xn2_done, tr2_ps, gw_sb, E, bank[7]).then_inc(logits_ps, 1)

            def ranks(g):
                pe.wait_ge(picks_ready, g + 1)
                for t in range(GT):
                    n = g * GT + t
                    pe.matmul(bank[7][:, t * E:(t + 1) * E], before[:, :], picks[:, n, :], start=True, stop=False)
                    mm = pe.matmul(bank[7][:, t * E:(t + 1) * E], ones[:, :], earlier[:, n, :], start=False, stop=True)
                mm.then_inc(rank_ps, 1)

            def bias2(g):
                pe.wait_ge(comb_ready, g + 1)
                pe.wait_ge(wT_sb, min(g + 2, NG))
                for t in range(GT):
                    mm = pe.transpose(bank[4][0:E, t * P:(t + 1) * P], comb[:, g % 2, t, :], ident[:, :])
                mm.then_inc(combT_ps, 1)
                pe.wait_ge(combT_sb, g + 1)
                for j in range(2):
                    pe.wait_ge(x1_ready, min(2 * (g + 1) + j + 1, 2 * NG - 1 + j))
                    for t in range(2):
                        mm = pe.matmul(bank[5 + j][:, t * D:(t + 1) * D], combT[:, 2 * j + t, :], b2_sb[:, :],
                                       start=True, stop=True)
                    mm.then_inc(b2_ps, 1)

            scores(0)
            for s in range(STEPS):
                if 0 <= s - 1 < NG:
                    attention(s - 1)
                if 0 <= s - 2 < NG:
                    logits(s - 2)
                if s + 1 < NG:
                    scores(s + 1)
                if 0 <= s - 2 < NG:
                    ranks(s - 2)
                    bias2(s - 2)
            pe.wait_ge(rank_read, NG)
            pe.matmul(bank[7][:, 0:E], ones[:, :], earlier[:, NT, :], start=True, stop=True).then_inc(count_ps, 1)

            def transpose_tile(i, s):
                pe.wait_ge(xg_in[s % NX], i // NX * 16 + 16 if isinstance(i, int) else (i - s) * (16 // NX) + s // NX * 16 + 16)
                if not (isinstance(i, int) and i < 2):
                    pe.wait_ge(xT_sb, i - 1)
                part = xg[:, s % NX, 0:D].bitcast(F16)
                tb = bank[6 + s % 2][:, 0:D].bitcast(F16)
                for q in range(2 * KC):
                    mm = pe.transpose(tb[:, q * P:(q + 1) * P], part[:, q * P:(q + 1) * P], ident16[:, :])
                mm.then_inc(xT_ps, 1)

            def fc1_operands(c, e):
                return [[w[:, bass.ds(e, 1), k, c * P:(c + 1) * P].rearrange("p a f -> p (a f)")
                         for w in (w1hi, w1lo)] for k in range(KC)]

            def fc2_operands(c, e):
                return [w[:, bass.ds(e, 1), c, :].rearrange("p a d -> p (a d)") for w in (w2hi, w2lo)]

            def fc1(i, s, c, ws):
                half = c // (FC // 2)
                if c == 0:
                    pe.wait_ge(xT_sb, i + 1)
                if c % (FC // 2) == 0 and not (isinstance(i, int) and i < 2):
                    pe.wait_ge(gelu_done, i * 2 + (half - 3))
                put = bank[2 * (s % 2) + half][:, c % (FC // 2) * P:(c % (FC // 2) + 1) * P]
                for k in range(KC):
                    hi, lo = ws[k]
                    for n, (w, x_part) in enumerate(((hi, 0), (hi, 1), (lo, 0))):
                        mm = pe.matmul(put, w, xT[:, s % 2, x_part, k, :],
                                       start=(k == 0 and n == 0), stop=(k == KC - 1 and n == 2))
                if c % (FC // 2) == FC // 2 - 1:
                    mm.then_inc(fc1_ps, 1)

            def fc2(i, s, c, ws):
                yb = bank[4 + s % 2][:, 0:D]
                if c == 0 and not (isinstance(i, int) and i < 2):
                    pe.wait_ge(y_ready, i - 1)
                if c % (FC // 2) == 0:
                    pe.wait_ge(lo_done, i * 2 + (c // (FC // 2) + 1))
                hp = hhi[s % 2][:, c * P:(c + 1) * P]
                lp = hlo[s % 2][:, c * P:(c + 1) * P]
                for n, (h, w) in enumerate(((hp, ws[0]), (hp, ws[1]), (lp, ws[0]))):
                    mm = pe.matmul(yb, h, w, start=(c == 0 and n == 0), stop=(c == FC - 1 and n == 2))
                if c == FC - 1:
                    mm.then_inc(y_ps, 1)

            def expert_of(i):
                return pe.value_load(te_i[0:1, bass.ds(i, 1)], min_val=0, max_val=E - 1)

            def tile(i, s, e, e1, e2, nxt=True):
                for c in range(FC):
                    back, e_b, c_b = (2, e2, c + FC // 2) if c < FC // 2 else (1, e1, c - FC // 2)
                    w1 = fc1_operands(c, e) if e is not None else None
                    w2 = fc2_operands(c_b, e_b) if e_b is not None else None
                    if w1:
                        for k in range(KC):
                            for w in w1[k]:
                                pe.lower_ap(w, for_matmul_weights=True)
                    if w2:
                        for w in w2:
                            pe.lower_ap(w)
                    if w1:
                        fc1(i, s, c, w1)
                    if w2:
                        fc2(i - back, s + NX - back, c_b, w2)
                    if c == 2 and nxt:
                        transpose_tile(i + 1, s + 1)

            pe.wait_ge(table_ready, 1)
            pe.wait_ge(w_hi, NU)
            pe.wait_ge(w_lo, NU)
            pe.wait_ge(b2_ps, 2 * NG)
            pe.wait_ge(init_ready, 2 * NG)
            transpose_tile(0, 0)
            e2, e1 = None, None
            for i in range(NX):
                e = expert_of(i)
                tile(i, i, e, e1, e2)
                e2, e1 = e1, e
            with pe.Fori(1, TILES // NX) as m:
                e2, e1 = expert_of(m * NX - 2), expert_of(m * NX - 1)
                for s in range(NX):
                    e = expert_of(m * NX + s)
                    tile(m * NX + s, s, e, e1, e2)
                    e2, e1 = e1, e
            tail = TILES // NX * NX
            e2, e1 = expert_of(tail - 2), expert_of(tail - 1)
            for i in range(tail, TILES + 2):
                e = expert_of(i) if i < TILES else None
                tile(i, i % NX, e, e1, e2, nxt=(i < TILES - 1))
                e2, e1 = e1, e

        @block.scalar
        def _(act):
            for dst, src in (
                (desc_sb[:, :], desc[:, :]),
                (wq_sb[:, :, :], w_q.rearrange("(c p) d -> p c d", p=P)),
                (bias_rows[E * FC:E * FC + KC, :], b_q.rearrange("(c p) -> c p", p=P)),
                (itok[:, :, :], token_sets.rearrange("(h p) k -> p h k", p=P)),
                (gcol[:, 0:1], g_xattn.rearrange("(a b) -> a b", a=1).to_broadcast([P, 1])),
                (gcol[:, 1:2], g_ffn.rearrange("(a b) -> a b", a=1).to_broadcast([P, 1])),
                (gw_sb[:, :, :], gate_w.rearrange("(c p) e -> p c e", p=P)),
                (gb_bc[:, :], gate_b.rearrange("(a e) -> a e", a=1).to_broadcast([P, E])),
                (alpha_bc[:, :], alpha.rearrange("(a e) -> a e", a=1).to_broadcast([P, E])),
                (b2_sb[:, :], fc2_b[:, :]),
                (bias_rows[0:E * FC, :], fc1_b.rearrange("e (f p) -> (e f) p", p=P)),
            ):
                act.dma_start(dst, src).then_inc(small_in, 16)
            act.dma_start(ctx_sb[:, :, :], ctx_sets.rearrange("b n d -> n b d")).then_inc(ctx_in, 16)
            act.wait_ge(small_in, 16 * NSMALL)
            act.activation(tg[:, :], gcol[:, :], ACT.Tanh).then_inc(gates_ready, 1)

            pairs = Count()

            def normalise(g, rstd, shift, done_sem, ps_sem, copied_sem):
                for t in range(GT):
                    n = g * GT + t
                    act.activation(xn[:, t, :], xs[:, n, :], ACT.Identity, bias=shift[:, n:n + 1],
                                   scale=rstd[:, n:n + 1]).then_inc(done_sem, 1)
                for j in range(2):
                    u = pairs.n
                    act.wait_ge(ps_sem, 2 * g + j + 1)
                    act.activation(xnT[:, u % 2, :, :, :].rearrange("p t k q -> p (t k q)"), bank[u % 2][:, :],
                                   ACT.Copy).then_inc(tr_pairs, 1)
                    pairs.up()

            def norm1(g):
                act.wait_ge(ln1, g + 1)
                if g >= 1:
                    if g >= 3:
                        act.wait_ge(logits_ps, g - 2)
                        act.wait_ge(row_ready, g - 2)
                    act.wait_ge(scores_ps, g)
                normalise(g, rstd1, shift1, xn1_done, tr1_ps, tr1_sb)

            def norm2(g):
                act.wait_ge(ln2, g + 1)
                act.wait_ge(scores_ps, min(g + 2, NG))
                if g >= 1:
                    act.wait_ge(logits_ps, g)
                    act.wait_ge(row_ready, g)
                if g >= 2:
                    act.wait_ge(scattered[g % 2], 16 * 2 * GT)
                normalise(g, rstd2, shift2, xn2_done, tr2_ps, tr1_sb)
                act.wait_ge(xn2_done, (g + 1) * GT)
                for t in range(GT):
                    op = act.activation(rows[:, g % 2, t, 0:P].bitcast(F16), xn[:, t, :], ACT.Copy)
                op.then_inc(hi_ready, 1)

            def weights_hi(u):
                act.wait_ge(w_in[u % NSTAGE], 16 * (u // NSTAGE + 1))
                act.activation(unit_parts(u)[0], wstage[:, u % NSTAGE, :], ACT.Copy, scale=W_SCALE).then_inc(w_hi, 1)

            norm1(0)
            for s in range(STEPS):
                if 0 <= s - 1 < NG:
                    act.wait_ge(wT_ps, s)
                    act.activation(wT[:, :, :].rearrange("n t p -> n (t p)"), bank[4][0:NS, :], ACT.Copy).then_inc(wT_sb, 1)
                if 0 <= s - 2 < NG:
                    norm2(s - 2)
                if s < NG:
                    act.wait_ge(diff_ready, s + 1)
                    act.activation(ediff[:, s % 2, :], diff[:, s % 2, :], ACT.Exp).then_inc(exp_ready, 1)
                if 0 <= s - 2 < NG:
                    act.wait_ge(gdiff_ready, s - 1)
                    act.activation(gediff[:, s % 2, :], gdiff[:, s % 2, :], ACT.Exp).then_inc(gexp_ready, 1)
                if s + 1 < NG:
                    norm1(s + 1)
                for u in range(unit_at[s], unit_at[s + 1]):
                    weights_hi(u)
                if 0 <= s - 2 < NG:
                    act.wait_ge(combT_ps, s - 1)
                    act.activation(combT[:, :, :].rearrange("e t p -> e (t p)"), bank[4][0:E, :], ACT.Copy).then_inc(combT_sb, 1)
                if 0 <= s - 3 < NG:
                    g = s - 3
                    act.wait_ge(init_ready, 2 * (g + 1))
                    act.dma_start(out_t[:, g * GT:(g + 1) * GT, :], xs[:, g * GT:(g + 1) * GT, :]).then_inc(out_init, 16)
            for u in range(unit_at[STEPS], NU):
                weights_hi(u)
            g = NG - 1
            act.wait_ge(init_ready, 2 * NG)
            act.dma_start(out_t[:, g * GT:(g + 1) * GT, :], xs[:, g * GT:(g + 1) * GT, :]).then_inc(out_init, 16)

            def gelu(i, s, half):
                if half == 0:
                    act.wait_ge(b1_ready, i + 1)
                act.wait_ge(fc1_ps, i * 2 + (half + 1))
                if not (isinstance(i, int) and i < 2):
                    act.wait_ge(lo_done, i * 2 + (half - 3))
                for c in range(FC // 2):
                    f = half * (FC // 2) + c
                    op = act.activation(h32[s % 2][:, f * P:(f + 1) * P],
                                        bank[2 * (s % 2) + half][:, c * P:(c + 1) * P], ACT.Gelu,
                                        bias=b1cur[:, s % NX, f:f + 1], scale=1.0 / (X_SCALE * W_SCALE))
                op.then_inc(gelu_done, 1)

            def weigh(i, s):
                act.wait_ge(cur_ready, i + 1)
                act.wait_ge(y_ps, i + 1)
                if not (isinstance(i, int) and i < 2):
                    act.wait_ge(added, i * 16 - 16)
                act.activation(y_sb[:, s % 2, :], bank[4 + s % 2][:, 0:D], ACT.Copy,
                               scale=wcur[:, s % NX:s % NX + 1]).then_inc(y_ready, 1)

            act.wait_ge(out_init, 16 * NG)
            def tile(i, s, first=False):
                gelu(i, s, 0)
                if not first:
                    weigh(i - 2, s + NX - 2)
                gelu(i, s, 1)

            for i in range(NX):
                tile(i, i, first=(i < 2))
            with act.Fori(1, TILES // NX) as m:
                for s in range(NX):
                    tile(m * NX + s, s)
            for i in range(TILES // NX * NX, TILES):
                tile(i, i % NX)
            for i in range(TILES - 2, TILES):
                weigh(i, i % NX)

        @block.vector
        def _(v):
            done = Count()

            v.memset(ones[:, :], 1.0).then_inc(vec_step, 1)
            v.memset(earlier[:, 0, :], 0.0)
            v.wait_ge(vec_step, done.up())
            v.wait_ge(small_in, 16 * NSMALL)
            v.wait_ge(pool_const, 3)
            v.wait_ge(b1T_ps, 1)
            v.tensor_copy(bias_cols[:, :], bank[4][:, 0:E * FC + KC]).then_inc(b1T_sb, 1)
            v.wait_ge(b1T_sb, 1)
            for c in range(KC):
                v.tensor_scalar(bq_bc[:, c, :], ones[:, :], bq_col[:, c:c + 1], None, ALU.mult)
            v.wait_ge(descT_ps, 1)
            v.tensor_copy(descT[:, :, :].rearrange("p c n -> p (c n)"), bank[2][:, 0:KC * NS]).then_inc(descT_sb, 1)
            v.tensor_copy(itok_f[:, :, :], itok[:, :, :]).then_inc(vec_step, 1)
            v.tensor_copy(iota64[:, :], iota_i[:, :]).then_inc(vec_step, 1)
            v.tensor_copy(iota_t[:, :], iota_ti[:, :]).then_inc(vec_step, 1)
            v.tensor_copy(part_f[:, :], part_i[:, :]).then_inc(vec_step, 1)
            v.tensor_copy(ident16[:, :], ident[:, :]).then_inc(vec_step, 1)
            v.wait_ge(vec_step, done.up(5))
            v.tensor_scalar(region[:, :], iota64[:, 0:E], float(CAP), None, ALU.mult).then_inc(vec_step, 1)
            for h in range(HALVES):
                v.tensor_scalar(maskbias[:, h, :], iota64[:, :], itok_f[:, h, 0:1], None, ALU.is_equal).then_inc(vec_step, 1)
            v.wait_ge(vec_step, done.up(3))
            for k in range(1, KSET):
                for h in range(HALVES):
                    v.scalar_tensor_tensor(out=maskbias[:, h, :], in0=iota64[:, :], scalar=itok_f[:, h, k:k + 1],
                                           in1=maskbias[:, h, :], op0=ALU.is_equal, op1=ALU.max).then_inc(vec_step, 1)
                v.wait_ge(vec_step, done.up(HALVES))
            v.tensor_scalar(maskbias[:, :, :], maskbias[:, :, :], -MASKED, MASKED, ALU.mult, ALU.add).then_inc(vec_step, 1)
            v.wait_ge(vec_step, done.up())
            v.wait_ge(proj_ps, 1)
            for h in range(HALVES):
                v.scalar_tensor_tensor(out=maskbias[:, h, :], in0=bank[3][:, 2 * NS:3 * NS], scalar=D ** -0.5,
                                       in1=maskbias[:, h, :], op0=ALU.mult, op1=ALU.add).then_inc(vec_step, 1)
            v.tensor_copy(proj[:, :, :].rearrange("p c n -> p (c n)"), bank[3][:, 0:KC * NS]).then_inc(proj_ready, 1)
            v.wait_ge(vec_step, done.up(HALVES))
            v.wait_ge(gates_ready, 1)

            def row_stats(g, tiles, mv, stats_done):
                for t in tiles:
                    v.bn_stats(stats[:, g * GT + t, :], xs[:, g * GT + t, :]).then_inc(vec_step, 1)
                v.wait_ge(vec_step, done.up(len(tiles)))
                for t in tiles:
                    v.bn_aggr(mv[:, g * GT + t, :], stats[:, g * GT + t, :]).then_inc(stats_done, 1)

            def norm1_stats(g):
                v.wait_ge(x_in[g], 16)
                row_stats(g, range(GT), mv1, stats1)

            def pick_sets(g):
                v.wait_ge(scores_ps, g + 1)
                v.scalar_tensor_tensor(
                    out=masked[:, :, :].rearrange("p (b h) n -> p b (h n)", h=HALVES),
                    in0=bank[2 + g % 2][:, 0:GT * NS].rearrange("p (b n) -> p b n", b=GT // HALVES), scalar=D ** -0.5,
                    in1=maskbias[:, :, :].rearrange("p h n -> p (h n)").unsqueeze(1).to_broadcast([P, GT // HALVES, HALVES * NS]),
                    op0=ALU.mult, op1=ALU.add).then_inc(scores_read, 1)
                v.wait_ge(scores_read, g + 1)
                for t in range(GT):
                    v.max(top8[:, g % 2, t, :], masked[:, t, :]).then_inc(vec_step, 1)
                v.wait_ge(vec_step, done.up(GT))
                v.tensor_tensor(diff[:, g % 2, :], top8[:, g % 2, :, 1], top8[:, g % 2, :, 0], ALU.subtract).then_inc(diff_ready, 1)
                for t in range(GT):
                    v.max_index(top8i[:, g % 2, t, :], top8[:, g % 2, t, :], masked[:, t, :]).then_inc(vec_step, 1)
                v.wait_ge(vec_step, done.up(GT))

            def softmax_pair(e2, den_, pair, gate):
                v.tensor_scalar(den_[:, :], e2, 1.0, None, ALU.add).then_inc(vec_step, 1)
                v.wait_ge(vec_step, done.up())
                v.reciprocal(den_[:, :], den_[:, :]).then_inc(vec_step, 1)
                v.wait_ge(vec_step, done.up())
                v.tensor_scalar(pair[:, :, 0], den_[:, :], gate, None, ALU.mult).then_inc(vec_step, 1)
                v.wait_ge(vec_step, done.up())
                v.tensor_tensor(pair[:, :, 1], e2, pair[:, :, 0], ALU.mult).then_inc(vec_step, 1)
                v.wait_ge(vec_step, done.up())

            def set_weights(g):
                v.tensor_copy(top2f[:, :, :], top8i[:, g % 2, :, 0:2]).then_inc(vec_step, 1)
                v.wait_ge(vec_step, done.up())
                v.wait_ge(exp_ready, g + 1)
                softmax_pair(ediff[:, g % 2, :], den, wpair, tg[:, 0:1])
                for t in range(GT):
                    for k in range(2):
                        v.tensor_scalar(wset[:, k, t, :], iota64[:, :], top2f[:, t, k:k + 1], wpair[:, t, k:k + 1],
                                        ALU.is_equal, ALU.mult).then_inc(vec_step, 1)
                v.wait_ge(vec_step, done.up(2 * GT))
                if g >= 1:
                    v.wait_ge(wT_ps, g)
                v.tensor_tensor(wsum[:, :, :], wset[:, 0, :, :], wset[:, 1, :, :], ALU.add).then_inc(wset_ready, 1)
                v.wait_ge(wset_ready, g + 1)

            def add_attention(g):
                for j in range(2):
                    v.wait_ge(attn_ps, 2 * g + j + 1)
                    pair = xs[:, g * GT + 2 * j:g * GT + 2 * j + 2, :].rearrange("p t d -> p (t d)")
                    v.tensor_tensor(pair, bank[5 + j][:, :], pair, ALU.add).then_inc(x1_ready, 1)
                    v.wait_ge(x1_ready, 2 * g + j + 1)
                    row_stats(g, range(2 * j, 2 * j + 2), mv2, stats2)

            def route(g):
                v.wait_ge(logits_ps, g + 1)
                v.scalar_tensor_tensor(out=logit[:, :, :], in0=bank[7][:, 0:GT * E].rearrange("p (t e) -> p t e", t=GT),
                                       scalar=1.0 / X_SCALE, in1=gb_bc[:, :].unsqueeze(1).to_broadcast([P, GT, E]),
                                       op0=ALU.mult, op1=ALU.add).then_inc(vec_step, 1)
                v.wait_ge(vec_step, done.up())
                for t in range(GT):
                    v.max(gtop[:, g % 2, t, :], logit[:, t, :]).then_inc(vec_step, 1)
                v.wait_ge(vec_step, done.up(GT))
                v.tensor_tensor(gdiff[:, g % 2, :], gtop[:, g % 2, :, 1], gtop[:, g % 2, :, 0], ALU.subtract).then_inc(gdiff_ready, 1)
                for t in range(GT):
                    v.max_index(gtopi[:, g % 2, t, :], gtop[:, g % 2, t, :], logit[:, t, :]).then_inc(vec_step, 1)
                v.wait_ge(vec_step, done.up(GT))
                v.tensor_copy(gtop2f[:, :, :], gtopi[:, g % 2, :, 0:2]).then_inc(vec_step, 1)
                v.wait_ge(vec_step, done.up())
                v.tensor_tensor(onehot[:, :, :, :].rearrange("p t k e -> p (t k) e"),
                                iota64[:, 0:E].unsqueeze(1).to_broadcast([P, GT * 2, E]),
                                gtop2f[:, :, :].rearrange("p t k -> p (t k)").unsqueeze(2).to_broadcast([P, GT * 2, E]),
                                ALU.is_equal).then_inc(vec_step, 1)
                v.wait_ge(vec_step, done.up())
                tiles = slice(g * GT, (g + 1) * GT)
                v.tensor_tensor(picks[:, tiles, :], onehot[:, :, 0, :], onehot[:, :, 1, :], ALU.add).then_inc(vec_step, 1)
                v.wait_ge(vec_step, done.up())
                for t in range(GT):
                    n = g * GT + t
                    v.tensor_tensor(earlier[:, n + 1, :], earlier[:, n, :], picks[:, n, :], ALU.add).then_inc(
                        picks_ready if t == GT - 1 else vec_step, 1)
                    if t < GT - 1:
                        v.wait_ge(vec_step, done.up())
                v.wait_ge(picks_ready, g + 1)

            def combine_weights(g):
                v.wait_ge(gexp_ready, g + 1)
                softmax_pair(gediff[:, g % 2, :], gden, gpair, tg[:, 1:2])
                v.tensor_tensor(oh_tmp[:, :, :, :].rearrange("p t k e -> p (t k) e"),
                                onehot[:, :, :, :].rearrange("p t k e -> p (t k) e"),
                                gpair[:, :, :].rearrange("p t k -> p (t k)").unsqueeze(2).to_broadcast([P, GT * 2, E]),
                                ALU.mult).then_inc(vec_step, 1)
                v.wait_ge(vec_step, done.up())
                v.tensor_tensor(comb[:, g % 2, :, :], oh_tmp[:, :, 0, :], oh_tmp[:, :, 1, :], ALU.add).then_inc(vec_step, 1)
                v.wait_ge(vec_step, done.up())
                v.tensor_tensor(comb[:, g % 2, :, :], comb[:, g % 2, :, :],
                                alpha_bc[:, :].unsqueeze(1).to_broadcast([P, GT, E]), ALU.mult).then_inc(comb_ready, 1)

            def slots(g):
                v.wait_ge(rank_ps, g + 1)
                v.tensor_tensor(rank[:, :, :], bank[7][:, 0:GT * E].rearrange("p (t e) -> p t e", t=GT),
                                region[:, :].unsqueeze(1).to_broadcast([P, GT, E]), ALU.add).then_inc(rank_read, 1)
                v.wait_ge(rank_read, g + 1)
                for k in range(2):
                    v.tensor_tensor(oh_tmp[:, :, k, :], onehot[:, :, k, :], rank[:, :, :], ALU.mult).then_inc(vec_step, 1)
                v.wait_ge(vec_step, done.up(2))
                v.tensor_reduce(slot_f[:, :, :].rearrange("p t k -> p (t k)"),
                                oh_tmp[:, :, :, :].rearrange("p t k e -> p (t k) e"), AX.X, ALU.add).then_inc(vec_step, 1)
                v.wait_ge(vec_step, done.up())
                v.wait_ge(comb_ready, g + 1)
                if g >= 2:
                    v.wait_ge(scattered[g % 2], 16 * 2 * GT)
                v.tensor_scalar(rows[:, g % 2, :, W_COMB:W_TOK].bitcast(F32), comb[:, g % 2, :, :],
                                1.0 / (H_SCALE * W_SCALE), None, ALU.mult)
                v.tensor_copy(slot_i[:, g, :, :], slot_f[:, :, :]).then_inc(slots_ready, 1)

            def start_output(g):
                for j in range(2):
                    v.wait_ge(b2_ps, 2 * g + j + 1)
                    v.wait_ge(xn2_done, (g + 1) * GT)
                    pair = xs[:, g * GT + 2 * j:g * GT + 2 * j + 2, :].rearrange("p t d -> p (t d)")
                    v.tensor_tensor(pair, bank[5 + j][:, :], pair, ALU.add).then_inc(init_ready, 1)

            def weights_lo(u):
                v.wait_ge(w_hi, u + 1)
                hi, lo = unit_parts(u)
                v.scalar_tensor_tensor(out=lo, in0=wstage[:, u % NSTAGE, :], scalar=W_SCALE, in1=hi,
                                       op0=ALU.mult, op1=ALU.subtract).then_inc(w_lo, 1)

            norm1_stats(0)
            norm1_stats(1)
            for s in range(STEPS):
                if s < NG:
                    pick_sets(s)
                if 0 <= s - 2 < NG:
                    route(s - 2)
                if s < NG:
                    set_weights(s)
                if 0 <= s - 2 < NG:
                    combine_weights(s - 2)
                if 0 <= s - 1 < NG:
                    add_attention(s - 1)
                if s + 2 < NG:
                    norm1_stats(s + 2)
                if 0 <= s - 2 < NG:
                    slots(s - 2)
                for u in range(unit_at[s], unit_at[s + 1]):
                    weights_lo(u)
                if 0 <= s - 2 < NG:
                    start_output(s - 2)

            v.wait_ge(count_ps, 1)
            v.tensor_copy(cnt[:, :], bank[7][:, 0:E]).then_inc(vec_step, 1)
            v.wait_ge(vec_step, done.up())
            v.tensor_scalar(cnt_i[:, :], cnt[:, :], float(P - 1), None, ALU.add).then_inc(vec_step, 1)
            v.wait_ge(vec_step, done.up())
            v.tensor_single_scalar(tl_i[:, :], cnt_i[:, :], 7, op=ALU.logical_shift_right).then_inc(vec_step, 1)
            v.wait_ge(vec_step, done.up())
            v.tensor_scalar(tl[:, :], tl_i[:, :], 1.0, None, ALU.max).then_inc(vec_step, 1)
            v.wait_ge(vec_step, done.up())
            v.tensor_scalar(pad_f[:, :], cnt[:, :], part_f[:, 0:1], None, ALU.add).then_inc(vec_step, 1)
            v.wait_ge(vec_step, done.up())
            v.scalar_tensor_tensor(out=pad_ok[:, :], in0=tl[:, :], scalar=float(P), in1=pad_f[:, :],
                                   op0=ALU.mult, op1=ALU.is_le).then_inc(vec_step, 1)
            v.tensor_tensor(pad_f[:, :], pad_f[:, :], region[:, :], ALU.add).then_inc(vec_step, 1)
            v.wait_ge(vec_step, done.up(2))
            v.scalar_tensor_tensor(out=pad_i[:, :], in0=pad_ok[:, :], scalar=float(NOWHERE), in1=pad_f[:, :],
                                   op0=ALU.mult, op1=ALU.max).then_inc(pads_ready, 1)
            v.tensor_tensor_scan(ctl[:, :], ones[:, 0:E], tl[:, :], 0.0, ALU.mult, ALU.add).then_inc(vec_step, 1)
            v.wait_ge(vec_step, done.up())
            v.tensor_tensor(over[:, :, :], ctl[0:1, :].unsqueeze(1).to_broadcast([1, TILES, E]),
                            iota_t[:, :].unsqueeze(2).to_broadcast([1, TILES, E]), ALU.is_le).then_inc(vec_step, 1)
            v.wait_ge(vec_step, done.up())
            v.tensor_tensor(over2[:, :, :], over[:, :, :], tl[0:1, :].unsqueeze(1).to_broadcast([1, TILES, E]),
                            ALU.mult).then_inc(vec_step, 1)
            v.tensor_reduce(te_f[:, :], over[:, :, :], AX.X, ALU.add).then_inc(vec_step, 1)
            v.wait_ge(vec_step, done.up(2))
            v.tensor_reduce(tc_f[:, :], over2[:, :, :], AX.X, ALU.add).then_inc(vec_step, 1)
            v.tensor_scalar(te_i[:, :], te_f[:, :], float(E - 1), None, ALU.min).then_inc(vec_step, 1)
            v.wait_ge(vec_step, done.up(2))
            v.tensor_tensor(tc_f[:, :], iota_t[:, :], tc_f[:, :], ALU.subtract).then_inc(vec_step, 1)
            v.wait_ge(vec_step, done.up())
            v.tensor_scalar(tc_f[:, :], tc_f[:, :], float(P), None, ALU.mult).then_inc(vec_step, 1)
            v.wait_ge(vec_step, done.up())
            v.scalar_tensor_tensor(out=tr_i[:, :], in0=te_f[:, :], scalar=float(CAP), in1=tc_f[:, :],
                                   op0=ALU.mult, op1=ALU.add).then_inc(table_ready, 1)
            for u in range(unit_at[STEPS], NU):
                weights_lo(u)

            def expert_of(i):
                return v.value_load(te_i[0:1, bass.ds(i, 1)], min_val=0, max_val=E - 1)

            def fetch(i, s, e):
                v.wait_ge(xT_ps, i + 1)
                if not (isinstance(i, int) and i < 2):
                    v.wait_ge(fc1_ps, i * 2 - 2)
                v.tensor_copy(xT[:, s % 2, :, :, :].rearrange("p a k q -> p (a k q)"),
                              bank[6 + s % 2][:, 0:D].bitcast(F16)).then_inc(xT_sb, 1)
                if not (isinstance(i, int) and i < NX):
                    v.wait_ge(gelu_done, i * 2 + (2 - 2 * NX))
                v.tensor_copy(b1cur[:, s % NX, :], b1T[:, bass.ds(e, 1), :].rearrange("p a f -> p (a f)")).then_inc(b1_ready, 1)

            def keep(i, s, e):
                if not (isinstance(i, int) and i < NX):
                    v.wait_ge(added, i * 16 + (16 - 16 * NX))
                v.tensor_copy(wcur[:, s % NX:s % NX + 1], xg[:, s % NX, bass.ds(e + W_COMB, 1)].bitcast(F32))
                v.tensor_copy(tokcur[:, s % NX:s % NX + 1], xg[:, s % NX, W_TOK:ROW].bitcast(U32)).then_inc(cur_ready, 1)

            def split(i, s, half):
                c = slice(half * (F // 2), (half + 1) * (F // 2))
                v.wait_ge(gelu_done, i * 2 + (half + 1))
                if not (isinstance(i, int) and i < 2):
                    v.wait_ge(y_ps, i - 1)
                v.tensor_scalar(hhi[s % 2][:, c], h32[s % 2][:, c], H_SCALE, None, ALU.mult).then_inc(hi_done, 1)
                v.wait_ge(hi_done, i * 2 + (half + 1))
                v.scalar_tensor_tensor(out=hlo[s % 2][:, c], in0=h32[s % 2][:, c], scalar=H_SCALE,
                                       in1=hhi[s % 2][:, c], op0=ALU.mult, op1=ALU.subtract).then_inc(lo_done, 1)

            def tile(i, s, e, e1, nxt=True, first=False):
                if nxt:
                    fetch(i + 1, s + 1, e)
                if not first:
                    keep(i - 1, s + NX - 1, e1)
                split(i, s, 0)
                split(i, s, 1)

            v.wait_ge(table_ready, 1)
            e0 = expert_of(0)
            fetch(0, 0, e0)
            es = [e0]
            for i in range(NX):
                es.append(expert_of(i + 1))
                tile(i, i, es[i + 1], es[i - 1], first=(i == 0))
            with v.Fori(1, TILES // NX) as m:
                es = [expert_of(m * NX - 1), expert_of(m * NX)]
                for s in range(NX):
                    es.append(expert_of(m * NX + (s + 1)))
                    tile(m * NX + s, s, es[s + 2], es[s])
            for i in range(TILES // NX * NX, TILES):
                nxt = i < TILES - 1
                tile(i, i % NX, expert_of(i + 1) if nxt else None, expert_of(i - 1), nxt=nxt)
            keep(TILES - 1, (TILES - 1) % NX, expert_of(TILES - 1))

        @block.gpsimd
        def _(pool):
            step = Count()
            pool.memset(ident[:, :], 1.0).then_inc(pool_step, 1)
            pool.memset(before[:, :], 1.0).then_inc(pool_step, 1)
            pool.memset(pad_row[:, :], 0).then_inc(pool_step, 1)
            pool.memset(neg_half[:, :], -0.5).then_inc(pool_step, 1)
            pool.wait_ge(pool_step, step.up(4))
            pool.affine_select(out=ident[:, :], in_=ident[:, :], pattern=[[-1, P]], base=0, channel_multiplier=1,
                               compare_op=ALU.is_equal, fill=0.0).then_inc(pool_const, 1)
            pool.affine_select(out=before[:, :], in_=before[:, :], pattern=[[1, P]], base=0, channel_multiplier=-1,
                               compare_op=ALU.is_gt, fill=0.0).then_inc(pool_step, 1)
            step.up()
            pool.iota(iota_i[:, :], pattern=[[1, NS]], base=0, channel_multiplier=0)
            pool.iota(iota_ti[:, :], pattern=[[1, TILES]], base=0, channel_multiplier=0)
            pool.iota(part_i[:, :], pattern=[[0, 1]], base=0, channel_multiplier=1).then_inc(pool_const, 1)
            pool.iota(pad_row[:, W_TOK:ROW], pattern=[[0, 1]], base=T, channel_multiplier=1).then_inc(pool_const, 1)
            pool.wait_ge(pool_const, 3)
            for k in range(SPARE):
                pool.dma_start(xsort[E * CAP + k * P:E * CAP + (k + 1) * P, :], pad_row[:, :]).then_inc(pads_out, 16)
            pool.dma_start(out[T:T + P, :], pad_row[:, 0:D].bitcast(F32)).then_inc(pad_out_init, 16)

            def rstd_shift(mv, rstd, shift, g, scale, stats_done, ln_done):
                r = slice(g * GT, (g + 1) * GT)
                pool.wait_ge(stats_done, (g + 1) * GT)
                pool.tensor_scalar(rstd[:, r], mv[:, r, 1], EPS, scale ** -2, ALU.add, ALU.mult).then_inc(pool_step, 1)
                pool.tensor_scalar(shift[:, r], mv[:, r, 0], -1.0, None, ALU.mult).then_inc(pool_step, 1)
                pool.wait_ge(pool_step, step.up(2))
                pool.tensor_tensor(rstd[:, r], rstd[:, r], neg_half[:, :], ALU.pow).then_inc(pool_step, 1)
                pool.wait_ge(pool_step, step.up())
                pool.tensor_tensor(shift[:, r], shift[:, r], rstd[:, r], ALU.mult).then_inc(ln_done, 1)

            for g in range(NG):
                rstd_shift(mv1, rstd1, shift1, g, 1.0, stats1, ln1)
            rstd_shift(mv2, rstd2, shift2, 0, X_SCALE, stats2, ln2)
            for g in range(NG):
                if g + 1 < NG:
                    rstd_shift(mv2, rstd2, shift2, g + 1, X_SCALE, stats2, ln2)
                if g >= 2:
                    pool.wait_ge(scattered[g % 2], 16 * 2 * GT)
                pool.wait_ge(hi_ready, g + 1)
                for t in range(GT):
                    pool.iota(rows[:, g % 2, t, W_TOK:ROW], pattern=[[0, 1]], base=(g * GT + t) * P,
                              channel_multiplier=1)
                    op = pool.tensor_tensor(rows[:, g % 2, t, P:2 * P].bitcast(F16), xn[:, t, :],
                                            rows[:, g % 2, t, 0:P].bitcast(F16), ALU.subtract)
                op.then_inc(row_ready, 1)
                pool.wait_ge(slots_ready, g + 1)
                pool.wait_ge(row_ready, g + 1)
                for t in range(GT):
                    for k in range(2):
                        pool.indirect_dma_start(
                            out=xsort[:, :], out_offset=bass.IndirectOffsetOnAxis(ap=slot_i[:, g, t, k:k + 1], axis=0),
                            in_=rows[:, g % 2, t, :], in_offset=None).then_inc(scattered[g % 2], 16)
            pool.wait_ge(pads_ready, 1)
            for e in range(E):
                pool.indirect_dma_start(
                    out=xsort[:, :], out_offset=bass.IndirectOffsetOnAxis(ap=pad_i[:, e:e + 1], axis=0),
                    in_=pad_row[:, :], in_offset=None, bounds_check=E * CAP + SPARE * P - 1,
                    oob_is_err=False).then_inc(pads_out, 16)
            pool.wait_ge(scattered[0], 16 * 4 * GT)
            pool.wait_ge(scattered[1], 16 * 4 * GT)
            pool.wait_ge(pads_out, 16 * (SPARE + E))
            pool.sem_inc(sorted_done, 1)

            def add_tile(i, s):
                pool.wait_ge(y_ready, i + 1)
                if not (isinstance(i, int) and i == 0):
                    pool.wait_ge(added, i * 16)
                pool.sem_inc(add_started, 1)
                pool.indirect_dma_start(
                    out=out[:, :], out_offset=bass.IndirectOffsetOnAxis(ap=tokcur[:, s:s + 1], axis=0),
                    in_=y_sb[:, s % 2, :], in_offset=None, compute_op=ALU.add).then_inc(added, 16)

            pool.wait_ge(out_init, 16 * NG)
            pool.wait_ge(pad_out_init, 16)
            for i in range(NX):
                add_tile(i, i)
            with pool.Fori(1, TILES // NX) as m:
                for s in range(NX):
                    add_tile(m * NX + s, s)
            for i in range(TILES // NX * NX, TILES):
                add_tile(i, i % NX)
            pool.wait_ge(added, TILES * 16)


_INS = ['x', 'ctx_2048', 'itok_Sx4_0_63', 'g_xattn', 'g_ffn', 'L0_xattn_desc_router', 'L0_xattn_W_q',
        'L0_xattn_b_q', 'L0_ffn_gate_w', 'L0_ffn_gate_b', 'L0_ffn_fc1_w', 'L0_ffn_fc1_b', 'L0_ffn_fc2_w',
        'L0_ffn_fc2_b', 'L0_ffn_alpha']


def kernel(**inputs):
    import numpy as _np
    import concourse.bacc as _bacc
    from concourse import mybir as _mybir
    from concourse.bass_utils import run_bass_kernel_spmd as _run

    nc = _bacc.Bacc("TRN2", target_bir_lowering=False, num_devices=1)
    arrays, args = {}, []
    for name in _INS:
        a = _np.ascontiguousarray(inputs[name])
        arrays[f"in_{name}_dram"] = a
        args.append(nc.dram_tensor(f"in_{name}_dram", a.shape, _mybir.dt.from_np(a.dtype), kind="ExternalInput").ap())
    shape = inputs['x'].shape
    tokens = shape[0] * shape[1]
    out = nc.dram_tensor("out_dram", [tokens + 128, shape[2]], _mybir.dt.float32, kind="ExternalOutput").ap()
    flamingo_block(nc, *args, out)
    r = _run(nc, [arrays], core_ids=[0])
    return r.results[0]["out_dram"][:tokens].reshape(shape)
```

```python
from contextlib import ExitStack

import concourse.bass as bass
from concourse import mybir

ALU = mybir.AluOpType
ACT = mybir.ActivationFunctionType
AX = mybir.AxisListType
F32 = mybir.dt.float32
F16 = mybir.dt.float16
I32 = mybir.dt.int32
U32 = mybir.dt.uint32

P = 128
X_SCALE = 16.0
W_SCALE = 128.0
H_SCALE = 16.0
MASKED = -1.0e30
EPS = 1e-5


class Count:

    def __init__(self):
        self.n = 0

    def up(self, by=1):
        self.n += by
        return self.n


def flamingo_block(nc, x, ctx_sets, token_sets, g_xattn, g_ffn, desc, w_q, b_q, gate_w, gate_b,
                   fc1_w, fc1_b, fc2_w, fc2_b, alpha, out):
    B, S, D = x.shape
    NS = ctx_sets.shape[1]
    KSET = token_sets.shape[1]
    E, _, F = fc1_w.shape
    T = B * S
    NT = T // P
    GT = 4
    NG = NT // GT
    KC = D // P
    FC = F // P
    HALVES = S // P
    CAP = T + P
    TILES = (2 * T - E) // P + E
    SPARE = TILES - 2 * T // P
    W_COMB = D
    W_TOK = W_COMB + E
    ROW = W_TOK + 1
    NU = 2 * E
    NSTAGE = 4
    NX = 4
    HEAD = 8
    UNROLL = 4
    LOOPS = (TILES - HEAD) // UNROLL
    assert KC == 2 and HALVES == 2 and D == 256 and NG == 4 and FC == 8 and TILES == 39

    xt = x.rearrange("b (h p) d -> p (b h) d", p=P)
    out_t = out[0:T, :].rearrange("(t p) d -> p t d", p=P)
    xsort = nc.dram_tensor("xsort", [E * CAP + SPARE * P, ROW], I32, kind="Internal").ap()

    with ExitStack() as stack:
        def sb(name, shape, dt=F32):
            return stack.enter_context(nc.sbuf_tensor(name, shape, dt))

        def sem(name):
            return stack.enter_context(nc.semaphore(name))

        w1hi = sb("w1hi", [P, E, KC, F], F16)
        w1lo = sb("w1lo", [P, E, KC, F], F16)
        w2hi = sb("w2hi", [P, E, FC, D], F16)
        w2lo = sb("w2lo", [P, E, FC, D], F16)
        wstage = sb("wstage", [P, 2, KC * F])
        stage_buf = [wstage[:, 0, :], wstage[:, 1, :],
                     w1hi[:, E - 2:E].rearrange("p e k f -> p (e k f)").bitcast(F32),
                     w2hi[:, E - 2:E].rearrange("p e f d -> p (e f d)").bitcast(F32)]
        arena = sb("arena", [P, NT, D])
        xs = arena
        xn = sb("xn", [P, GT, D])
        xn1 = w2lo[:, E - 1].rearrange("p f d -> p (f d)").bitcast(F32).rearrange("p (t d) -> p t d", t=GT)
        xnT = sb("xnT", [P, 2, 2, KC, P])
        rows = sb("rows", [P, 2, GT, ROW], I32)
        early = rows[:, :, :, :].rearrange("p g t w -> p (g t w)").bitcast(F32)
        wq_sb = early[:, 0:2 * D].rearrange("p (c d) -> p c d", c=KC)
        bq_bc = early[:, 2 * D:3 * D].rearrange("p (c q) -> p c q", c=KC)
        desc_sb = early[0:NS, 3 * D:4 * D]
        bias_rows = early[0:E * FC + KC, 4 * D:4 * D + P]
        ctx_buf = sb("ctx_buf", [P, B, D])
        ctx_sb = ctx_buf[0:NS, :, :]
        descT = sb("descT", [P, KC, NS])
        proj = sb("proj", [P, KC, NS])
        itok = sb("itok", [P, HALVES, KSET], I32)
        itok_f = sb("itok_f", [P, HALVES, KSET])
        maskbias = sb("maskbias", [P, HALVES, NS])
        gcol = sb("gcol", [P, 2])
        tg = sb("tg", [P, 2])
        tg_gelu = sb("tg_gelu", [P, 2])
        gw_sb = sb("gw_sb", [P, KC, E])
        gb_bc = sb("gb_bc", [P, E])
        alpha_bc = sb("alpha_bc", [P, E])
        b2_sb = sb("b2_sb", [E, D])
        bias_cols = sb("bias_cols", [P, E * FC + KC])
        b1T = bias_cols[:, 0:E * FC].rearrange("p (e f) -> p e f", e=E)
        bq_col = bias_cols[:, E * FC:E * FC + KC]
        ident = sb("ident", [P, P])
        ident16 = sb("ident16", [P, P], F16)
        ones = sb("ones", [P, P])
        before = sb("before", [P, P])
        iota_i = sb("iota_i", [P, NS], I32)
        iota64 = sb("iota64", [P, NS])
        iota_ti = sb("iota_ti", [1, TILES], I32)
        iota_t = sb("iota_t", [1, TILES])
        region = sb("region", [P, E])
        pad_row = sb("pad_row", [P, ROW], I32)
        stats = sb("stats", [P, NT, 6])
        neg_half = sb("neg_half", [P, GT])
        mv1 = sb("mv1", [P, NT, 2])
        rstd1 = sb("rstd1", [P, NT])
        shift1 = sb("shift1", [P, NT])
        mv2 = sb("mv2", [P, NT, 2])
        rstd2 = sb("rstd2", [P, NT])
        shift2 = sb("shift2", [P, NT])
        masked = sb("masked", [P, GT, NS])
        top8 = sb("top8", [P, 2, GT, 8])
        top8i = sb("top8i", [P, 2, GT, 8], U32)
        top2f = sb("top2f", [P, GT, 2])
        diff = sb("diff", [P, 2, GT])
        ediff = sb("ediff", [P, 2, GT])
        den = sb("den", [P, GT])
        wpair = sb("wpair", [P, GT, 2])
        wset = sb("wset", [P, 2, GT, NS])
        wsum = sb("wsum", [P, GT, NS])
        wT = sb("wT", [NS, GT, P])
        logit = sb("logit", [P, GT, E])
        gtop = sb("gtop", [P, 2, GT, 8])
        gtopi = sb("gtopi", [P, 2, GT, 8], U32)
        gtop2f = sb("gtop2f", [P, GT, 2])
        gdiff = sb("gdiff", [P, 2, GT])
        gediff = sb("gediff", [P, 2, GT])
        gden = sb("gden", [P, GT])
        gpair = sb("gpair", [P, GT, 2])
        onehot = sb("onehot", [P, GT, 2, E])
        oh_tmp = sb("oh_tmp", [P, GT, 2, E])
        alpha2 = sb("alpha2", [P, GT, 2])
        comb = sb("comb", [P, 2, GT, E])
        combT = sb("combT", [E, GT, P])
        picks = sb("picks", [P, NT, E])
        earlier = sb("earlier", [P, NT + 1, E])
        rank = sb("rank", [P, GT, E])
        slot_f = sb("slot_f", [P, GT, 2])
        slot_i = sb("slot_i", [P, NG, GT, 2], U32)
        cnt = sb("cnt", [P, E])
        cnt_i = sb("cnt_i", [P, E], I32)
        tl_i = sb("tl_i", [P, E], I32)
        tl = sb("tl", [P, E])
        ctl = sb("ctl", [P, E])
        pad_at = sb("pad_at", [1, E], I32)
        over = wset[0:1, :, :, :].rearrange("a k t n -> a (k t n)")[:, 0:TILES * E].rearrange("a (i e) -> a i e", e=E)
        over2 = wT[0:1, :, :].rearrange("a t p -> a (t p)")[:, 0:TILES * E].rearrange("a (i e) -> a i e", e=E)
        te_f = sb("te_f", [1, TILES])
        tc_f = sb("tc_f", [1, TILES])
        tr_f = sb("tr_f", [1, TILES])
        te_i = sb("te_i", [1, TILES], I32)
        tr_i = sb("tr_i", [1, TILES], I32)
        xg = ctx_buf[:, :, :].rearrange("p b d -> p (b d)")[:, 0:NX * ROW].bitcast(I32).rearrange(
            "p (s w) -> p s w", s=NX)
        b1cur = sb("b1cur", [P, NX, FC])
        wcur = sb("wcur", [P, NX])
        tokcur = sb("tokcur", [P, NX], U32)
        xT = xnT[:, 0, :, :, :].rearrange("p t k q -> p (t k q)").bitcast(F16).rearrange(
            "p (s a k q) -> p s a k q", s=2, a=2, k=KC)
        y_sb = xn[:, 0:2, :]
        flat = arena[:, :, :].rearrange("p t d -> p (t d)")
        h32 = [flat[:, j * F:(j + 1) * F] for j in range(2)]
        hhi = [flat[:, 2 * F + j * F // 2:2 * F + (j + 1) * F // 2].bitcast(F16) for j in range(2)]
        hlo = [flat[:, 3 * F + j * F // 2:3 * F + (j + 1) * F // 2].bitcast(F16) for j in range(2)]

        bank = [stack.enter_context(nc.psum_tensor(f"bank{i}", [P, 512], F32)) for i in range(8)]

        x_in = [sem(f"x_in{g}") for g in range(NG)]
        small_in = sem("small_in")
        small2_in = sem("small2_in")
        ctx_in = sem("ctx_in")
        w_in = [sem(f"w_in{s}") for s in range(NSTAGE)]
        w_hi = sem("w_hi")
        w_lo = sem("w_lo")
        pool_const = sem("pool_const")
        pool_step = sem("pool_step")
        vec_const = sem("vec_const")
        vec_step = sem("vec_step")
        gates_ready = sem("gates_ready")
        descT_ps = sem("descT_ps")
        descT_sb = sem("descT_sb")
        bq_ready = sem("bq_ready")
        proj_ps = sem("proj_ps")
        proj_ready = sem("proj_ready")
        stats1 = sem("stats1")
        stats2 = sem("stats2")
        ln1 = sem("ln1")
        xn1_done = sem("xn1_done")
        tr1_ps = sem("tr1_ps")
        pair_used = sem("pair_used")
        tr_pairs = sem("tr_pairs")
        scores_read = sem("scores_read")
        diff_ready = sem("diff_ready")
        exp_ready = sem("exp_ready")
        wset_ready = sem("wset_ready")
        wT_ps = sem("wT_ps")
        wT_sb = sem("wT_sb")
        attn_ps = sem("attn_ps")
        x1_ready = sem("x1_ready")
        ln2 = sem("ln2")
        xn2_done = sem("xn2_done")
        tr2_ps = sem("tr2_ps")
        hi_ready = sem("hi_ready")
        row_ready = sem("row_ready")
        logits_read = sem("logits_read")
        gdiff_ready = sem("gdiff_ready")
        gexp_ready = sem("gexp_ready")
        comb_ready = sem("comb_ready")
        picks_ready = sem("picks_ready")
        rank_ps = sem("rank_ps")
        rank_read = sem("rank_read")
        slots_ready = sem("slots_ready")
        combT_ps = sem("combT_ps")
        combT_sb = sem("combT_sb")
        b2_ps = sem("b2_ps")
        init_ready = sem("init_ready")
        out_init = sem("out_init")
        pad_out_init = sem("pad_out_init")
        scattered = [sem(f"scattered{r}") for r in range(2)]
        count_ps = sem("count_ps")
        pads_ready = sem("pads_ready")
        spare_out = sem("spare_out")
        pads_out = sem("pads_out")
        table_ready = sem("table_ready")
        b1T_ps = sem("b1T_ps")
        b1T_sb = sem("b1T_sb")
        xg_in = [sem(f"xg_in{s}") for s in range(NX)]
        b1_ready = sem("b1_ready")
        cur_ready = sem("cur_ready")
        xT_ps = sem("xT_ps")
        xT_sb = sem("xT_sb")
        fc1_ps = sem("fc1_ps")
        gelu_done = sem("gelu_done")
        hi_done = sem("hi_done")
        lo_done = sem("lo_done")
        y_ps = sem("y_ps")
        y_ready = sem("y_ready")
        add_started = sem("add_started")
        added = sem("added")

        NSMALL, NSMALL2 = 5, 6
        xn2_of = [xn] * (NG - 1) + [xn1]

        def unit_parts(u):
            e = u // 2
            if u % 2 == 0:
                return w1hi[:, e].rearrange("p k f -> p (k f)"), w1lo[:, e].rearrange("p k f -> p (k f)")
            return w2hi[:, e].rearrange("p k f -> p (k f)"), w2lo[:, e].rearrange("p k f -> p (k f)")

        STEPS = NG + 3
        UNITS = [1, 1, 1, 2, 2, 1, 2]
        LATE = [1, 1, 1, 1, 1, 1, 0, 0]
        unit_at = [sum(UNITS[:s]) for s in range(STEPS + 1)]
        late_at = [unit_at[-1] + sum(LATE[:i]) for i in range(HEAD + 1)]
        assert late_at[-1] == NU and all(late_at[i] >= min(2 * (i + 1), NU) for i in range(HEAD))

        stage_of = [u % NSTAGE if u < NU - 4 else u % 2 for u in range(NU)]
        before_in = [max([w for w in range(u) if stage_of[w] == stage_of[u]], default=None) for u in range(NU)]
        nth_in = [stage_of[:u + 1].count(stage_of[u]) for u in range(NU)]

        pair_at = {(1, 0): 0}
        for s in range(STEPS):
            if 0 <= s - 2 < NG:
                pair_at[(2, s - 2)] = 2 * len(pair_at)
            if s + 1 < NG:
                pair_at[(1, s + 1)] = 2 * len(pair_at)

        block = stack.enter_context(nc.Block())

        @block.sync
        def _(sp):
            def load_unit(u):
                e, s = u // 2, stage_of[u]
                if before_in[u] is not None:
                    sp.wait_ge(w_hi, before_in[u] + 1)
                    sp.wait_ge(w_lo, before_in[u] + 1)
                if u % 2 == 0:
                    src = fc1_w[e].rearrange("(k p) f -> p k f", p=P)
                    dst = stage_buf[s].rearrange("p (k f) -> p k f", k=KC)
                else:
                    src = fc2_w[e].rearrange("(k p) d -> p k d", p=P)
                    dst = stage_buf[s].rearrange("p (k d) -> p k d", k=FC)
                sp.dma_start(dst, src).then_inc(w_in[s], 16)

            def load_tokens(g):
                sp.dma_start(xs[:, g * GT:(g + 1) * GT, :], xt[:, g * GT:(g + 1) * GT, :]).then_inc(x_in[g], 16)

            load_tokens(0)
            for dst, src in (
                (gcol[:, 0:1], g_xattn.rearrange("(a b) -> a b", a=1).to_broadcast([P, 1])),
                (gcol[:, 1:2], g_ffn.rearrange("(a b) -> a b", a=1).to_broadcast([P, 1])),
                (gw_sb[:, :, :], gate_w.rearrange("(c p) e -> p c e", p=P)),
                (gb_bc[:, :], gate_b.rearrange("(a e) -> a e", a=1).to_broadcast([P, E])),
                (alpha_bc[:, :], alpha.rearrange("(a e) -> a e", a=1).to_broadcast([P, E])),
                (b2_sb[:, :], fc2_b[:, :]),
            ):
                sp.dma_start(dst, src).then_inc(small2_in, 16)
            load_tokens(1)
            sp.dma_start(ctx_sb[:, :, :], ctx_sets.rearrange("b n d -> n b d")).then_inc(ctx_in, 16)
            load_tokens(2)
            load_tokens(3)
            sp.wait_ge(small_in, 16 * NSMALL)
            sp.wait_ge(small2_in, 16 * NSMALL2)
            for u in range(NSTAGE):
                load_unit(u)
            sp.wait_ge(pool_const, 3)
            for k in range(SPARE):
                sp.dma_start(xsort[E * CAP + k * P:E * CAP + (k + 1) * P, :], pad_row[:, :]).then_inc(spare_out, 16)
            sp.dma_start(out[T:T + P, :], pad_row[:, 0:D].bitcast(F32)).then_inc(pad_out_init, 16)
            for u in range(NSTAGE, unit_at[-1]):
                load_unit(u)
            sp.wait_ge(pads_ready, 1)
            for e in range(E):
                at = sp.value_load(pad_at[0:1, e:e + 1], min_val=e * CAP, max_val=e * CAP + T)
                sp.dma_start(xsort[bass.ds(at, P), :], pad_row[:, :]).then_inc(pads_out, 16)

            def load_tile(i, s):
                row = sp.value_load(tr_i[0:1, bass.ds(i, 1)], min_val=0, max_val=E * CAP + (SPARE - 1) * P)
                sp.dma_start(xg[:, s, :], xsort[bass.ds(row, P), :]).then_inc(xg_in[s], 16)

            sp.wait_ge(table_ready, 1)
            for r in range(2):
                sp.wait_ge(scattered[r], 16 * 4 * GT)
            sp.wait_ge(spare_out, 16 * SPARE)
            sp.wait_ge(pads_out, 16 * E)
            for i in range(NX):
                load_tile(i, i)
            u = unit_at[-1]
            while before_in[u] < unit_at[-1]:
                load_unit(u)
                u += 1
            for i in range(NX, HEAD):
                sp.wait_ge(cur_ready, i - NX + 1)
                load_tile(i, i % NX)
                while u < NU and before_in[u] < late_at[i - NX + 1]:
                    load_unit(u)
                    u += 1
            assert u == NU
            with sp.Fori(HEAD // NX, TILES // NX) as m:
                for s in range(NX):
                    sp.wait_ge(cur_ready, m * NX + (s + 1 - NX))
                    load_tile(m * NX + s, s)
            for i in range(TILES // NX * NX, TILES):
                sp.wait_ge(cur_ready, i - NX + 1)
                load_tile(i, i % NX)

        @block.tensor
        def _(pe):
            pe.wait_ge(small_in, 16 * NSMALL)
            pe.wait_ge(pool_const, 1)
            for c in range(KC):
                mm = pe.transpose(bank[2][:, c * NS:(c + 1) * NS], desc_sb[:, c * P:(c + 1) * P], ident[0:NS, 0:NS])
            mm.then_inc(descT_ps, 1)
            nb = E * FC + KC
            pe.transpose(bank[4][:, 0:nb], bias_rows[:, :], ident[0:nb, 0:nb]).then_inc(b1T_ps, 1)
            pe.wait_ge(descT_sb, 1)
            for k in range(KC):
                for c in range(KC):
                    pe.matmul(bank[3][:, k * NS:(k + 1) * NS], wq_sb[:, c, k * P:(k + 1) * P], descT[:, c, :],
                              start=(c == 0), stop=(c == KC - 1))
            pe.wait_ge(bq_ready, 1)
            for c in range(KC):
                mm = pe.matmul(bank[3][:, 2 * NS:3 * NS], bq_bc[:, c, :], descT[:, c, :],
                               start=(c == 0), stop=(c == KC - 1))
            mm.then_inc(proj_ps, 1)

            def transposed_pairs(ln, g, rows_in, done_sem, ps_sem, rhs, n, put):
                base = pair_at[(ln, g)]

                def products(j):
                    pe.wait_ge(tr_pairs, base + j + 1)
                    for t in range(2):
                        q = 2 * j + t
                        for k in range(KC):
                            mm = pe.matmul(put[:, q * n:(q + 1) * n], xnT[:, (base + j) % 2, t, k, :], rhs[:, k, :],
                                           start=(k == 0), stop=(k == KC - 1))
                    mm.then_inc(pair_used, 1)

                for j in range(2):
                    pe.wait_ge(done_sem, g * GT + 2 * j + 2)
                    if base + j >= 2:
                        pe.wait_ge(tr_pairs, base + j - 1)
                    for t in range(2):
                        for k in range(KC):
                            mm = pe.transpose(bank[(base + j) % 2][:, (t * KC + k) * P:(t * KC + k + 1) * P],
                                              rows_in[:, 2 * j + t, k * P:(k + 1) * P], ident[:, :])
                    mm.then_inc(ps_sem, 1)
                if ln == 1 and g == 0:
                    pe.wait_ge(proj_ready, 1)
                if ln == 2 and g >= 1:
                    pe.wait_ge(rank_read, g)
                products(0)
                products(1)

            def scores(g):
                if g >= 2:
                    pe.wait_ge(scores_read, g - 1)
                transposed_pairs(1, g, xn1, xn1_done, tr1_ps, proj, NS, bank[2 + g % 2])

            def attention(g):
                pe.wait_ge(wset_ready, g + 1)
                if g == 0:
                    pe.wait_ge(b1T_sb, 1)
                if g >= 3:
                    pe.wait_ge(combT_sb, g - 2)
                for t in range(GT):
                    mm = pe.transpose(bank[4][0:NS, t * P:(t + 1) * P], wsum[:, t, :], ident[:, :])
                mm.then_inc(wT_ps, 1)
                pe.wait_ge(wT_sb, g + 1)
                if g == 0:
                    pe.wait_ge(ctx_in, 16)
                for j in range(2):
                    if g == 1:
                        pe.wait_ge(x1_ready, j + 1)
                    if g == 2:
                        pe.wait_ge(x1_ready, 2 + j + 1)
                    if g >= 3:
                        pe.wait_ge(init_ready, 2 * (g - 3) + j + 1)
                    for t in range(2):
                        q = 2 * j + t
                        mm = pe.matmul(bank[5 + j][:, t * D:(t + 1) * D], wT[:, q, :],
                                       ctx_sb[:, (g * GT + q) // HALVES, :], start=True, stop=True)
                    mm.then_inc(attn_ps, 1)

            def logits(g):
                if g == 0:
                    pe.wait_ge(small2_in, 16 * NSMALL2)
                transposed_pairs(2, g, xn2_of[g], xn2_done, tr2_ps, gw_sb, E, bank[7])

            def ranks(g):
                pe.wait_ge(picks_ready, g + 1)
                if g == NG - 1:
                    pe.matmul(bank[7][:, GT * E:(GT + 1) * E], ones[:, :], earlier[:, NT, :],
                              start=True, stop=True).then_inc(count_ps, 1)
                tiles = slice(g * GT, (g + 1) * GT)
                pe.matmul(bank[7][:, 0:GT * E], before[:, :], picks[:, tiles, :].rearrange("p t e -> p (t e)"),
                          start=True, stop=False)
                pe.matmul(bank[7][:, 0:GT * E], ones[:, :], earlier[:, tiles, :].rearrange("p t e -> p (t e)"),
                          start=False, stop=True).then_inc(rank_ps, 1)

            def bias2(g):
                pe.wait_ge(comb_ready, g + 1)
                pe.wait_ge(wT_sb, min(g + 3, NG))
                for t in range(GT):
                    mm = pe.transpose(bank[4][0:E, t * P:(t + 1) * P], comb[:, g % 2, t, :], ident[:, :])
                mm.then_inc(combT_ps, 1)
                pe.wait_ge(combT_sb, g + 1)
                for j in range(2):
                    pe.wait_ge(x1_ready, 2 * min(g + 2, NG - 1) + j + 1)
                    if g + 2 >= NG:
                        pe.wait_ge(init_ready, 2 * (g - 1) + j + 1)
                    for t in range(2):
                        mm = pe.matmul(bank[5 + j][:, t * D:(t + 1) * D], combT[:, 2 * j + t, :], b2_sb[:, :],
                                       start=True, stop=True)
                    mm.then_inc(b2_ps, 1)

            scores(0)
            for s in range(STEPS):
                if 0 <= s - 1 < NG:
                    attention(s - 1)
                if 0 <= s - 2 < NG - 1:
                    logits(s - 2)
                if s + 1 < NG:
                    scores(s + 1)
                if s == NG + 1:
                    ranks(NG - 1)
                if 0 <= s - 3 < NG:
                    bias2(s - 3)
                if 0 <= s - 2 < NG - 1:
                    ranks(s - 2)
                if s == NG:
                    logits(NG - 1)

            def transpose_tile(i, s):
                pe.wait_ge(xg_in[s % NX], i // NX * 16 + 16 if isinstance(i, int) else (i - s % NX) * (16 // NX) + 16)
                if not (isinstance(i, int) and i < 2):
                    pe.wait_ge(xT_sb, i - 1)
                part = xg[:, s % NX, 0:D].bitcast(F16)
                tb = bank[6 + s % 2][:, 0:D].bitcast(F16)
                for q in range(2 * KC):
                    mm = pe.transpose(tb[:, q * P:(q + 1) * P], part[:, q * P:(q + 1) * P], ident16[:, :])
                mm.then_inc(xT_ps, 1)

            def fc1_operands(c, e):
                return [[w[:, bass.ds(e, 1), k, c * P:(c + 1) * P].rearrange("p a f -> p (a f)")
                         for w in (w1hi, w1lo)] for k in range(KC)]

            def fc2_operands(c, e):
                return [w[:, bass.ds(e, 1), c, :].rearrange("p a d -> p (a d)") for w in (w2hi, w2lo)]

            def fc1(i, s, c, ws):
                half = c // (FC // 2)
                if c == 0:
                    pe.wait_ge(xT_sb, i + 1)
                if c % (FC // 2) == 0 and not (isinstance(i, int) and i < 2):
                    pe.wait_ge(gelu_done, i * 2 + (half - 3))
                put = bank[2 * (s % 2) + half][:, c % (FC // 2) * P:(c % (FC // 2) + 1) * P]
                for k in range(KC):
                    hi, lo = ws[k]
                    for n, (w, x_part) in enumerate(((hi, 0), (hi, 1), (lo, 0))):
                        mm = pe.matmul(put, w, xT[:, s % 2, x_part, k, :],
                                       start=(k == 0 and n == 0), stop=(k == KC - 1 and n == 2))
                if c % (FC // 2) == FC // 2 - 1:
                    mm.then_inc(fc1_ps, 1)

            def fc2(i, s, c, ws):
                yb = bank[4 + s % 2][:, 0:D]
                if c == 0 and not (isinstance(i, int) and i < 2):
                    pe.wait_ge(y_ready, i - 1)
                if c % (FC // 2) == 0:
                    pe.wait_ge(lo_done, i * 2 + (c // (FC // 2) + 1))
                hp = hhi[s % 2][:, c * P:(c + 1) * P]
                lp = hlo[s % 2][:, c * P:(c + 1) * P]
                for n, (h, w) in enumerate(((hp, ws[0]), (hp, ws[1]), (lp, ws[0]))):
                    mm = pe.matmul(yb, h, w, start=(c == 0 and n == 0), stop=(c == FC - 1 and n == 2))
                if c == FC - 1:
                    mm.then_inc(y_ps, 1)

            def experts(i, n):
                return nc.values_load_multi_w_load_instructions(
                    te_i[0:1, bass.ds(i, n)], engines=[mybir.EngineType.PE], min_val=0, max_val=E - 1,
                    skip_runtime_bounds_check_because="table() keeps the experts within 0 .. E - 1")[1]

            def tile(i, s, e, e1, e2, nxt=True):
                for c in range(FC):
                    back, e_b, c_b = (2, e2, c + FC // 2) if c < FC // 2 else (1, e1, c - FC // 2)
                    w1 = fc1_operands(c, e) if e is not None else None
                    w2 = fc2_operands(c_b, e_b) if e_b is not None else None
                    if w1:
                        for k in range(KC):
                            for w in w1[k]:
                                pe.lower_ap(w, for_matmul_weights=True)
                    if w2:
                        for w in w2:
                            pe.lower_ap(w)
                    if w1:
                        fc1(i, s, c, w1)
                    if w2:
                        fc2(i - back, s + NX - back, c_b, w2)
                    if c == 2 and nxt:
                        transpose_tile(i + 1, s + 1)

            pe.wait_ge(table_ready, 1)
            pe.wait_ge(b2_ps, 2 * NG)
            pe.wait_ge(init_ready, 2 * NG)
            transpose_tile(0, 0)
            es = [None, None, *experts(0, HEAD)]
            for i in range(HEAD):
                pe.wait_ge(w_hi, 2 * (i + 1))
                pe.wait_ge(w_lo, 2 * (i + 1))
                tile(i, i % NX, es[i + 2], es[i + 1], es[i])
            with pe.Fori(0, LOOPS) as m:
                es = experts(m * UNROLL + (HEAD - 2), UNROLL + 2)
                for s in range(UNROLL):
                    tile(m * UNROLL + (HEAD + s), s % NX, es[s + 2], es[s + 1], es[s])
            tail = HEAD + LOOPS * UNROLL
            es = [*experts(tail - 2, TILES - tail + 2), None, None]
            for i in range(tail, TILES + 2):
                tile(i, i % NX, es[i - tail + 2], es[i - tail + 1], es[i - tail], nxt=(i < TILES - 1))

        @block.scalar
        def _(act):
            for dst, src in (
                (desc_sb[:, :], desc[:, :]),
                (wq_sb[:, :, :], w_q.rearrange("(c p) d -> p c d", p=P)),
                (bias_rows[E * FC:E * FC + KC, :], b_q.rearrange("(c p) -> c p", p=P)),
                (bias_rows[0:E * FC, :], fc1_b.rearrange("e (f p) -> (e f) p", p=P)),
                (itok[:, :, :], token_sets.rearrange("(h p) k -> p h k", p=P)),
            ):
                act.dma_start(dst, src).then_inc(small_in, 16)
            def normalise(g, dst, rstd, shift, done_sem):
                for t in range(GT):
                    n = g * GT + t
                    act.activation(dst[:, t, :], xs[:, n, :], ACT.Identity, bias=shift[:, n:n + 1],
                                   scale=rstd[:, n:n + 1]).then_inc(done_sem, 1)

            def copy_pairs(ln, g, ps_sem):
                for j in range(2):
                    u = pair_at[(ln, g)] + j
                    act.wait_ge(ps_sem, 2 * g + j + 1)
                    if u >= 2:
                        act.wait_ge(pair_used, u - 1)
                    act.activation(xnT[:, u % 2, :, :, :].rearrange("p t k q -> p (t k q)"), bank[u % 2][:, :],
                                   ACT.Copy).then_inc(tr_pairs, 1)

            def norm1(g):
                act.wait_ge(ln1, g + 1)
                if g >= 1:
                    act.wait_ge(tr1_ps, 2 * g)
                normalise(g, xn1, rstd1, shift1, xn1_done)
                copy_pairs(1, g, tr1_ps)

            def norm2(g):
                act.wait_ge(ln2, g + 1)
                if g == NG - 1:
                    act.wait_ge(tr1_ps, 2 * NG)
                elif g >= 1:
                    act.wait_ge(tr2_ps, 2 * g)
                    act.wait_ge(row_ready, g)
                normalise(g, xn2_of[g], rstd2, shift2, xn2_done)

            def rows_hi(g):
                act.wait_ge(xn2_done, (g + 1) * GT)
                if g >= 2:
                    act.wait_ge(scattered[g % 2], 16 * 2 * GT)
                act.activation(rows[:, g % 2, :, 0:P].bitcast(F16), xn2_of[g][:, :, :], ACT.Copy).then_inc(hi_ready, 1)

            def weights_hi(u):
                act.wait_ge(w_in[stage_of[u]], 16 * nth_in[u])
                if u == NU - 4:
                    act.wait_ge(w_lo, u)
                act.activation(unit_parts(u)[0], stage_buf[stage_of[u]], ACT.Copy, scale=W_SCALE).then_inc(w_hi, 1)

            def store_rows(g):
                act.wait_ge(init_ready, 2 * (g + 1))
                act.dma_start(out_t[:, g * GT:(g + 1) * GT, :], xs[:, g * GT:(g + 1) * GT, :]).then_inc(out_init, 16)

            norm1(0)
            act.wait_ge(small2_in, 16 * NSMALL2)
            act.activation(tg[:, :], gcol[:, :], ACT.Tanh).then_inc(gates_ready, 1)
            for s in range(STEPS):
                if s < NG:
                    act.wait_ge(diff_ready, s + 1)
                    act.activation(ediff[:, s % 2, :], diff[:, s % 2, :], ACT.Exp).then_inc(exp_ready, 1)
                if 0 <= s - 1 < NG:
                    act.wait_ge(wT_ps, s)
                    act.activation(wT[:, :, :].rearrange("n t p -> n (t p)"), bank[4][0:NS, :], ACT.Copy).then_inc(wT_sb, 1)
                if 0 <= s - 2 < NG - 1:
                    norm2(s - 2)
                    copy_pairs(2, s - 2, tr2_ps)
                if s + 1 < NG:
                    norm1(s + 1)
                if 0 <= s - 2 < NG:
                    rows_hi(s - 2)
                if 0 <= s - 3 < NG:
                    act.wait_ge(combT_ps, s - 2)
                    act.activation(combT[:, :, :].rearrange("e t p -> e (t p)"), bank[4][0:E, :], ACT.Copy).then_inc(combT_sb, 1)
                if s == NG:
                    norm2(NG - 1)
                units = list(range(unit_at[s], unit_at[s + 1]))
                for u in units[:1]:
                    weights_hi(u)
                if 0 <= s - 2 < NG:
                    act.wait_ge(gdiff_ready, s - 1)
                    act.activation(gediff[:, s % 2, :], gdiff[:, s % 2, :], ACT.Exp).then_inc(gexp_ready, 1)
                if s == NG:
                    copy_pairs(2, NG - 1, tr2_ps)
                for u in units[1:]:
                    weights_hi(u)
                if 0 <= s - 4 < NG:
                    store_rows(s - 4)
            store_rows(NG - 1)
            act.activation(tg_gelu[:, :], gcol[:, :], ACT.Gelu)

            def gelu(i, s, half):
                if half == 0:
                    act.wait_ge(b1_ready, i + 1)
                act.wait_ge(fc1_ps, i * 2 + (half + 1))
                if not (isinstance(i, int) and i < 2):
                    act.wait_ge(lo_done, i * 2 + (half - 3))
                for c in range(FC // 2):
                    f = half * (FC // 2) + c
                    op = act.activation(h32[s % 2][:, f * P:(f + 1) * P],
                                        bank[2 * (s % 2) + half][:, c * P:(c + 1) * P], ACT.Gelu,
                                        bias=b1cur[:, s % NX, f:f + 1], scale=1.0 / (X_SCALE * W_SCALE))
                op.then_inc(gelu_done, 1)

            def weigh(i, s):
                act.wait_ge(cur_ready, i + 1)
                act.wait_ge(y_ps, i + 1)
                if not (isinstance(i, int) and i < 2):
                    act.wait_ge(added, i * 16 - 16)
                act.activation(y_sb[:, s % 2, :], bank[4 + s % 2][:, 0:D], ACT.Copy,
                               scale=wcur[:, s % NX:s % NX + 1]).then_inc(y_ready, 1)

            act.wait_ge(out_init, 16 * NG)
            def tile(i, s, first=False):
                gelu(i, s, 0)
                if not first:
                    weigh(i - 2, s + NX - 2)
                gelu(i, s, 1)

            for i in range(HEAD):
                tile(i, i % NX, first=(i < 2))
                for u in range(late_at[i], late_at[i + 1]):
                    weights_hi(u)
            with act.Fori(0, LOOPS) as m:
                for s in range(UNROLL):
                    tile(m * UNROLL + (HEAD + s), s % NX)
            for i in range(HEAD + LOOPS * UNROLL, TILES):
                tile(i, i % NX)
            for i in range(TILES - 2, TILES):
                weigh(i, i % NX)

        @block.vector
        def _(v):
            done = Count()

            def row_stats(g, tiles, mv, stats_done):
                for t in tiles:
                    v.bn_stats(stats[:, g * GT + t, :], xs[:, g * GT + t, :]).then_inc(vec_step, 1)
                v.wait_ge(vec_step, done.up(len(tiles)))
                for t in tiles:
                    v.bn_aggr(mv[:, g * GT + t, :], stats[:, g * GT + t, :]).then_inc(stats_done, 1)

            def norm1_stats(g):
                v.wait_ge(x_in[g], 16)
                row_stats(g, range(GT), mv1, stats1)

            v.memset(ones[:, :], 1.0).then_inc(vec_step, 1)
            v.memset(earlier[:, 0, :], 0.0)
            v.wait_ge(vec_step, done.up())
            norm1_stats(0)
            v.wait_ge(small_in, 16 * NSMALL)
            v.wait_ge(pool_const, 3)
            v.wait_ge(descT_ps, 1)
            v.tensor_copy(descT[:, :, :].rearrange("p c n -> p (c n)"), bank[2][:, 0:KC * NS]).then_inc(descT_sb, 1)
            v.wait_ge(b1T_ps, 1)
            v.tensor_copy(bias_cols[:, :], bank[4][:, 0:E * FC + KC]).then_inc(b1T_sb, 1)
            v.wait_ge(b1T_sb, 1)
            for c in range(KC):
                op = v.tensor_scalar(bq_bc[:, c, :], ones[:, :], bq_col[:, c:c + 1], None, ALU.mult)
            op.then_inc(bq_ready, 1)
            v.tensor_copy(itok_f[:, :, :], itok[:, :, :]).then_inc(vec_step, 1)
            v.tensor_copy(iota64[:, :], iota_i[:, :]).then_inc(vec_step, 1)
            v.tensor_copy(iota_t[:, :], iota_ti[:, :]).then_inc(vec_step, 1)
            v.tensor_copy(ident16[:, :], ident[:, :]).then_inc(vec_step, 1)
            v.wait_ge(vec_step, done.up(4))
            v.tensor_scalar(region[:, :], iota64[:, 0:E], float(CAP), None, ALU.mult).then_inc(vec_step, 1)
            for h in range(HALVES):
                v.tensor_scalar(maskbias[:, h, :], iota64[:, :], itok_f[:, h, 0:1], None, ALU.is_equal).then_inc(vec_step, 1)
            v.wait_ge(vec_step, done.up(3))
            for k in range(1, KSET):
                for h in range(HALVES):
                    v.scalar_tensor_tensor(out=maskbias[:, h, :], in0=iota64[:, :], scalar=itok_f[:, h, k:k + 1],
                                           in1=maskbias[:, h, :], op0=ALU.is_equal, op1=ALU.max).then_inc(vec_step, 1)
                v.wait_ge(vec_step, done.up(HALVES))
            v.tensor_scalar(maskbias[:, :, :], maskbias[:, :, :], -MASKED, MASKED, ALU.mult, ALU.add).then_inc(vec_step, 1)
            v.wait_ge(vec_step, done.up())
            v.wait_ge(proj_ps, 1)
            for h in range(HALVES):
                v.scalar_tensor_tensor(out=maskbias[:, h, :], in0=bank[3][:, 2 * NS:3 * NS], scalar=D ** -0.5,
                                       in1=maskbias[:, h, :], op0=ALU.mult, op1=ALU.add).then_inc(vec_step, 1)
            v.tensor_copy(proj[:, :, :].rearrange("p c n -> p (c n)"), bank[3][:, 0:KC * NS]).then_inc(proj_ready, 1)
            v.wait_ge(vec_step, done.up(HALVES))
            def pick_sets(g):
                v.wait_ge(pair_used, pair_at[(1, g)] + 2)
                v.scalar_tensor_tensor(
                    out=masked[:, :, :].rearrange("p (b h) n -> p b (h n)", h=HALVES),
                    in0=bank[2 + g % 2][:, 0:GT * NS].rearrange("p (b n) -> p b n", b=GT // HALVES), scalar=D ** -0.5,
                    in1=maskbias[:, :, :].rearrange("p h n -> p (h n)").unsqueeze(1).to_broadcast([P, GT // HALVES, HALVES * NS]),
                    op0=ALU.mult, op1=ALU.add).then_inc(scores_read, 1)
                v.wait_ge(scores_read, g + 1)
                for t in range(GT):
                    v.max(top8[:, g % 2, t, :], masked[:, t, :]).then_inc(vec_step, 1)
                v.wait_ge(vec_step, done.up(GT))
                v.tensor_tensor(diff[:, g % 2, :], top8[:, g % 2, :, 1], top8[:, g % 2, :, 0], ALU.subtract).then_inc(diff_ready, 1)
                for t in range(GT):
                    v.max_index(top8i[:, g % 2, t, :], top8[:, g % 2, t, :], masked[:, t, :]).then_inc(vec_step, 1)
                v.wait_ge(vec_step, done.up(GT))

            def softmax_pair(e2, den_, pair, gate):
                v.tensor_scalar(den_[:, :], e2, 1.0, None, ALU.add).then_inc(vec_step, 1)
                v.wait_ge(vec_step, done.up())
                v.reciprocal(den_[:, :], den_[:, :]).then_inc(vec_step, 1)
                v.wait_ge(vec_step, done.up())
                v.tensor_scalar(pair[:, :, 0], den_[:, :], gate, None, ALU.mult).then_inc(vec_step, 1)
                v.wait_ge(vec_step, done.up())
                v.tensor_tensor(pair[:, :, 1], e2, pair[:, :, 0], ALU.mult).then_inc(vec_step, 1)
                v.wait_ge(vec_step, done.up())

            def set_weights(g):
                v.tensor_copy(top2f[:, :, :], top8i[:, g % 2, :, 0:2]).then_inc(vec_step, 1)
                v.wait_ge(vec_step, done.up())
                v.wait_ge(exp_ready, g + 1)
                if g == 0:
                    v.wait_ge(gates_ready, 1)
                    v.wait_ge(small2_in, 16 * NSMALL2)
                softmax_pair(ediff[:, g % 2, :], den, wpair, tg[:, 0:1])
                for t in range(GT):
                    for k in range(2):
                        v.tensor_scalar(wset[:, k, t, :], iota64[:, :], top2f[:, t, k:k + 1], wpair[:, t, k:k + 1],
                                        ALU.is_equal, ALU.mult).then_inc(vec_step, 1)
                v.wait_ge(vec_step, done.up(2 * GT))
                if g >= 1:
                    v.wait_ge(wT_ps, g)
                v.tensor_tensor(wsum[:, :, :], wset[:, 0, :, :], wset[:, 1, :, :], ALU.add).then_inc(wset_ready, 1)
                v.wait_ge(wset_ready, g + 1)

            def add_attention(g):
                for j in range(2):
                    v.wait_ge(attn_ps, 2 * g + j + 1)
                    pair = xs[:, g * GT + 2 * j:g * GT + 2 * j + 2, :].rearrange("p t d -> p (t d)")
                    v.tensor_tensor(pair, bank[5 + j][:, :], pair, ALU.add).then_inc(x1_ready, 1)
                    v.wait_ge(x1_ready, 2 * g + j + 1)
                    row_stats(g, range(2 * j, 2 * j + 2), mv2, stats2)

            def route(g):
                v.wait_ge(pair_used, pair_at[(2, g)] + 2)
                v.scalar_tensor_tensor(out=logit[:, :, :], in0=bank[7][:, 0:GT * E].rearrange("p (t e) -> p t e", t=GT),
                                       scalar=1.0 / X_SCALE, in1=gb_bc[:, :].unsqueeze(1).to_broadcast([P, GT, E]),
                                       op0=ALU.mult, op1=ALU.add).then_inc(vec_step, 1)
                v.wait_ge(vec_step, done.up())
                for t in range(GT):
                    v.max(gtop[:, g % 2, t, :], logit[:, t, :]).then_inc(vec_step, 1)
                v.wait_ge(vec_step, done.up(GT))
                v.tensor_tensor(gdiff[:, g % 2, :], gtop[:, g % 2, :, 1], gtop[:, g % 2, :, 0], ALU.subtract).then_inc(gdiff_ready, 1)
                for t in range(GT):
                    v.max_index(gtopi[:, g % 2, t, :], gtop[:, g % 2, t, :], logit[:, t, :]).then_inc(vec_step, 1)
                v.wait_ge(vec_step, done.up(GT))
                v.tensor_copy(gtop2f[:, :, :], gtopi[:, g % 2, :, 0:2]).then_inc(vec_step, 1)
                v.wait_ge(vec_step, done.up())
                v.tensor_tensor(onehot[:, :, :, :].rearrange("p t k e -> p (t k) e"),
                                iota64[:, 0:E].unsqueeze(1).to_broadcast([P, GT * 2, E]),
                                gtop2f[:, :, :].rearrange("p t k -> p (t k)").unsqueeze(2).to_broadcast([P, GT * 2, E]),
                                ALU.is_equal).then_inc(vec_step, 1)
                v.wait_ge(vec_step, done.up())
                tiles = slice(g * GT, (g + 1) * GT)
                v.tensor_tensor(picks[:, tiles, :], onehot[:, :, 0, :], onehot[:, :, 1, :], ALU.add).then_inc(vec_step, 1)
                v.wait_ge(vec_step, done.up())
                for t in range(GT):
                    n = g * GT + t
                    v.tensor_tensor(earlier[:, n + 1, :], earlier[:, n, :], picks[:, n, :], ALU.add).then_inc(
                        picks_ready if t == GT - 1 else vec_step, 1)
                    if t < GT - 1:
                        v.wait_ge(vec_step, done.up())
                v.wait_ge(picks_ready, g + 1)

            def combine_weights(g):
                v.wait_ge(gexp_ready, g + 1)
                softmax_pair(gediff[:, g % 2, :], gden, gpair, tg[:, 1:2])
                v.tensor_tensor(oh_tmp[:, :, :, :].rearrange("p t k e -> p (t k) e"),
                                onehot[:, :, :, :].rearrange("p t k e -> p (t k) e"),
                                gpair[:, :, :].rearrange("p t k -> p (t k)").unsqueeze(2).to_broadcast([P, GT * 2, E]),
                                ALU.mult).then_inc(vec_step, 1)
                v.wait_ge(vec_step, done.up())
                if g >= 2:
                    v.wait_ge(combT_ps, g - 1)
                v.tensor_tensor(comb[:, g % 2, :, :], oh_tmp[:, :, 0, :], oh_tmp[:, :, 1, :], ALU.add).then_inc(vec_step, 1)
                v.wait_ge(vec_step, done.up())
                v.tensor_tensor(comb[:, g % 2, :, :], comb[:, g % 2, :, :],
                                alpha_bc[:, :].unsqueeze(1).to_broadcast([P, GT, E]), ALU.mult).then_inc(comb_ready, 1)

            def slots(g):
                v.wait_ge(rank_ps, g + 1)
                v.tensor_tensor(rank[:, :, :], bank[7][:, 0:GT * E].rearrange("p (t e) -> p t e", t=GT),
                                region[:, :].unsqueeze(1).to_broadcast([P, GT, E]), ALU.add).then_inc(rank_read, 1)
                v.wait_ge(rank_read, g + 1)
                for k in range(2):
                    v.tensor_tensor(oh_tmp[:, :, k, :], onehot[:, :, k, :], rank[:, :, :], ALU.mult).then_inc(vec_step, 1)
                v.wait_ge(vec_step, done.up(2))
                v.tensor_reduce(slot_f[:, :, :].rearrange("p t k -> p (t k)"),
                                oh_tmp[:, :, :, :].rearrange("p t k e -> p (t k) e"), AX.X, ALU.add).then_inc(vec_step, 1)
                v.wait_ge(vec_step, done.up())
                v.wait_ge(comb_ready, g + 1)
                if g >= 2:
                    v.wait_ge(scattered[g % 2], 16 * 2 * GT)
                v.tensor_scalar(rows[:, g % 2, :, W_COMB:W_TOK].bitcast(F32), comb[:, g % 2, :, :],
                                1.0 / (H_SCALE * W_SCALE), None, ALU.mult)
                v.tensor_copy(slot_i[:, g, :, :], slot_f[:, :, :]).then_inc(slots_ready, 1)

            def start_output(g):
                for j in range(2):
                    v.wait_ge(b2_ps, 2 * g + j + 1)
                    v.wait_ge(xn2_done, (g + 1) * GT)
                    pair = xs[:, g * GT + 2 * j:g * GT + 2 * j + 2, :].rearrange("p t d -> p (t d)")
                    v.tensor_tensor(pair, bank[5 + j][:, :], pair, ALU.add).then_inc(init_ready, 1)

            def weights_lo(u):
                v.wait_ge(w_hi, u + 1)
                if u == NU - 1:
                    v.wait_ge(row_ready, NG)
                hi, lo = unit_parts(u)
                v.scalar_tensor_tensor(out=lo, in0=stage_buf[stage_of[u]], scalar=W_SCALE, in1=hi,
                                       op0=ALU.mult, op1=ALU.subtract).then_inc(w_lo, 1)

            def table():
                v.wait_ge(count_ps, 1)
                v.tensor_copy(cnt[:, :], bank[7][:, GT * E:(GT + 1) * E]).then_inc(vec_step, 1)
                v.wait_ge(vec_step, done.up())
                v.tensor_tensor(pad_at[:, :], cnt[0:1, :], region[0:1, :], ALU.add).then_inc(pads_ready, 1)
                v.tensor_scalar(cnt_i[:, :], cnt[:, :], float(P - 1), None, ALU.add).then_inc(vec_step, 1)
                v.wait_ge(vec_step, done.up())
                v.tensor_single_scalar(tl_i[:, :], cnt_i[:, :], 7, op=ALU.logical_shift_right).then_inc(vec_step, 1)
                v.wait_ge(vec_step, done.up())
                v.tensor_scalar(tl[:, :], tl_i[:, :], 1.0, None, ALU.max).then_inc(vec_step, 1)
                v.wait_ge(vec_step, done.up())
                v.tensor_tensor_scan(ctl[:, :], ones[:, 0:E], tl[:, :], 0.0, ALU.mult, ALU.add).then_inc(vec_step, 1)
                v.wait_ge(vec_step, done.up())
                v.tensor_tensor(over[:, :, :], ctl[0:1, :].unsqueeze(1).to_broadcast([1, TILES, E]),
                                iota_t[:, :].unsqueeze(2).to_broadcast([1, TILES, E]), ALU.is_le).then_inc(vec_step, 1)
                v.wait_ge(vec_step, done.up())
                v.tensor_tensor(over2[:, :, :], over[:, :, :], tl[0:1, :].unsqueeze(1).to_broadcast([1, TILES, E]),
                                ALU.mult).then_inc(vec_step, 1)
                v.tensor_reduce(te_f[:, :], over[:, :, :], AX.X, ALU.add).then_inc(vec_step, 1)
                v.wait_ge(vec_step, done.up(2))
                v.tensor_reduce(tc_f[:, :], over2[:, :, :], AX.X, ALU.add).then_inc(vec_step, 1)
                v.tensor_scalar(te_i[:, :], te_f[:, :], float(E - 1), None, ALU.min).then_inc(vec_step, 1)
                v.wait_ge(vec_step, done.up(2))
                v.tensor_tensor(tc_f[:, :], iota_t[:, :], tc_f[:, :], ALU.subtract).then_inc(vec_step, 1)
                v.wait_ge(vec_step, done.up())
                v.tensor_scalar(tc_f[:, :], tc_f[:, :], float(P), None, ALU.mult).then_inc(vec_step, 1)
                v.wait_ge(vec_step, done.up())
                v.scalar_tensor_tensor(out=tr_i[:, :], in0=te_f[:, :], scalar=float(CAP), in1=tc_f[:, :],
                                       op0=ALU.mult, op1=ALU.add).then_inc(table_ready, 1)

            norm1_stats(1)
            for s in range(STEPS):
                if s < NG:
                    pick_sets(s)
                    set_weights(s)
                if 0 <= s - 1 < NG:
                    add_attention(s - 1)
                if s + 2 < NG:
                    norm1_stats(s + 2)
                if 0 <= s - 2 < NG:
                    route(s - 2)
                units = list(range(unit_at[max(s - 1, 0)], unit_at[s]))
                for u in units[:1]:
                    weights_lo(u)
                if 0 <= s - 2 < NG:
                    combine_weights(s - 2)
                    slots(s - 2)
                if s == NG + 1:
                    table()
                for u in units[1:] + (list(range(unit_at[s], unit_at[s + 1])) if s == STEPS - 1 else []):
                    weights_lo(u)
                if 0 <= s - 3 < NG:
                    start_output(s - 3)

            def expert_of(i):
                return v.value_load(te_i[0:1, bass.ds(i, 1)], min_val=0, max_val=E - 1)

            def fetch(i, s, e):
                v.wait_ge(xT_ps, i + 1)
                if not (isinstance(i, int) and i < 2):
                    v.wait_ge(fc1_ps, i * 2 - 2)
                v.tensor_copy(xT[:, s % 2, :, :, :].rearrange("p a k q -> p (a k q)"),
                              bank[6 + s % 2][:, 0:D].bitcast(F16)).then_inc(xT_sb, 1)
                if not (isinstance(i, int) and i < NX):
                    v.wait_ge(gelu_done, i * 2 + (2 - 2 * NX))
                v.tensor_copy(b1cur[:, s % NX, :], b1T[:, bass.ds(e, 1), :].rearrange("p a f -> p (a f)")).then_inc(b1_ready, 1)

            def keep(i, s, e):
                if not (isinstance(i, int) and i < NX):
                    v.wait_ge(added, i * 16 + (16 - 16 * NX))
                v.tensor_copy(wcur[:, s % NX:s % NX + 1], xg[:, s % NX, bass.ds(e + W_COMB, 1)].bitcast(F32))
                v.tensor_copy(tokcur[:, s % NX:s % NX + 1], xg[:, s % NX, W_TOK:ROW].bitcast(U32)).then_inc(cur_ready, 1)

            def split(i, s, half):
                c = slice(half * (F // 2), (half + 1) * (F // 2))
                v.wait_ge(gelu_done, i * 2 + (half + 1))
                if not (isinstance(i, int) and i < 2):
                    v.wait_ge(y_ps, i - 1)
                v.tensor_scalar(hhi[s % 2][:, c], h32[s % 2][:, c], H_SCALE, None, ALU.mult).then_inc(hi_done, 1)
                v.wait_ge(hi_done, i * 2 + (half + 1))
                v.scalar_tensor_tensor(out=hlo[s % 2][:, c], in0=h32[s % 2][:, c], scalar=H_SCALE,
                                       in1=hhi[s % 2][:, c], op0=ALU.mult, op1=ALU.subtract).then_inc(lo_done, 1)

            def tile(i, s, e, e1, nxt=True, first=False):
                if nxt:
                    fetch(i + 1, s + 1, e)
                if not first:
                    keep(i - 1, s + NX - 1, e1)
                split(i, s, 0)
                split(i, s, 1)

            v.wait_ge(table_ready, 1)
            e0 = expert_of(0)
            fetch(0, 0, e0)
            es = [e0]
            for i in range(HEAD):
                es.append(expert_of(i + 1))
                tile(i, i % NX, es[i + 1], es[i - 1], first=(i == 0))
                for u in range(late_at[i], late_at[i + 1]):
                    weights_lo(u)
            with v.Fori(0, LOOPS) as m:
                es = [expert_of(m * UNROLL + (HEAD - 1)), expert_of(m * UNROLL + HEAD)]
                for s in range(UNROLL):
                    es.append(expert_of(m * UNROLL + (HEAD + s + 1)))
                    tile(m * UNROLL + (HEAD + s), s % NX, es[s + 2], es[s])
            for i in range(HEAD + LOOPS * UNROLL, TILES):
                nxt = i < TILES - 1
                tile(i, i % NX, expert_of(i + 1) if nxt else None, expert_of(i - 1), nxt=nxt)
            keep(TILES - 1, (TILES - 1) % NX, expert_of(TILES - 1))

        @block.gpsimd
        def _(pool):
            step = Count()
            pool.memset(ident[:, :], 1.0).then_inc(pool_step, 1)
            pool.memset(before[:, :], 1.0).then_inc(pool_step, 1)
            pool.memset(pad_row[:, :], 0).then_inc(pool_step, 1)
            pool.memset(neg_half[:, :], -0.5).then_inc(pool_step, 1)
            pool.wait_ge(pool_step, step.up(4))
            pool.affine_select(out=ident[:, :], in_=ident[:, :], pattern=[[-1, P]], base=0, channel_multiplier=1,
                               compare_op=ALU.is_equal, fill=0.0).then_inc(pool_const, 1)
            pool.affine_select(out=before[:, :], in_=before[:, :], pattern=[[1, P]], base=0, channel_multiplier=-1,
                               compare_op=ALU.is_gt, fill=0.0).then_inc(pool_step, 1)
            step.up()
            pool.iota(iota_i[:, :], pattern=[[1, NS]], base=0, channel_multiplier=0)
            pool.iota(iota_ti[:, :], pattern=[[1, TILES]], base=0, channel_multiplier=0).then_inc(pool_const, 1)
            pool.iota(pad_row[:, W_TOK:ROW], pattern=[[0, 1]], base=T, channel_multiplier=1).then_inc(pool_const, 1)

            def rstd_shift(mv, rstd, shift, g, scale, stats_done, ln_done):
                r = slice(g * GT, (g + 1) * GT)
                pool.wait_ge(stats_done, (g + 1) * GT)
                pool.tensor_scalar(rstd[:, r], mv[:, r, 1], EPS, scale ** -2, ALU.add, ALU.mult).then_inc(pool_step, 1)
                pool.tensor_scalar(shift[:, r], mv[:, r, 0], -1.0, None, ALU.mult).then_inc(pool_step, 1)
                pool.wait_ge(pool_step, step.up(2))
                pool.tensor_tensor(rstd[:, r], rstd[:, r], neg_half[:, :], ALU.pow).then_inc(pool_step, 1)
                pool.wait_ge(pool_step, step.up())
                pool.tensor_tensor(shift[:, r], shift[:, r], rstd[:, r], ALU.mult).then_inc(ln_done, 1)

            def rows_lo(g):
                if g >= 2:
                    pool.wait_ge(scattered[g % 2], 16 * 2 * GT)
                pool.wait_ge(hi_ready, g + 1)
                for t in range(GT):
                    pool.iota(rows[:, g % 2, t, W_TOK:ROW], pattern=[[0, 1]], base=(g * GT + t) * P,
                              channel_multiplier=1)
                pool.tensor_tensor(rows[:, g % 2, :, P:2 * P].bitcast(F16), xn2_of[g][:, :, :],
                                   rows[:, g % 2, :, 0:P].bitcast(F16), ALU.subtract).then_inc(row_ready, 1)

            def scatter(g):
                pool.wait_ge(slots_ready, g + 1)
                pool.wait_ge(row_ready, g + 1)
                for t in range(GT):
                    for k in range(2):
                        pool.indirect_dma_start(
                            out=xsort[:, :], out_offset=bass.IndirectOffsetOnAxis(ap=slot_i[:, g, t, k:k + 1], axis=0),
                            in_=rows[:, g % 2, t, :], in_offset=None).then_inc(scattered[g % 2], 16)

            rstd_shift(mv1, rstd1, shift1, 0, 1.0, stats1, ln1)
            rstd_shift(mv1, rstd1, shift1, 1, 1.0, stats1, ln1)
            for s in range(STEPS):
                if 0 <= s - 1 < NG:
                    rstd_shift(mv2, rstd2, shift2, s - 1, X_SCALE, stats2, ln2)
                if s + 2 < NG:
                    rstd_shift(mv1, rstd1, shift1, s + 2, 1.0, stats1, ln1)
                if 0 <= s - 2 < NG:
                    rows_lo(s - 2)
                    scatter(s - 2)

            def add_tile(i, s):
                pool.wait_ge(y_ready, i + 1)
                if not (isinstance(i, int) and i == 0):
                    pool.wait_ge(added, i * 16)
                pool.sem_inc(add_started, 1)
                pool.indirect_dma_start(
                    out=out[:, :], out_offset=bass.IndirectOffsetOnAxis(ap=tokcur[:, s:s + 1], axis=0),
                    in_=y_sb[:, s % 2, :], in_offset=None, compute_op=ALU.add).then_inc(added, 16)

            pool.wait_ge(out_init, 16 * NG)
            pool.wait_ge(pad_out_init, 16)
            for i in range(NX):
                add_tile(i, i)
            with pool.Fori(1, TILES // NX) as m:
                for s in range(NX):
                    add_tile(m * NX + s, s)
            for i in range(TILES // NX * NX, TILES):
                add_tile(i, i % NX)
            pool.wait_ge(added, TILES * 16)


_INS = ['x', 'ctx_2048', 'itok_Sx4_0_63', 'g_xattn', 'g_ffn', 'L0_xattn_desc_router', 'L0_xattn_W_q',
        'L0_xattn_b_q', 'L0_ffn_gate_w', 'L0_ffn_gate_b', 'L0_ffn_fc1_w', 'L0_ffn_fc1_b', 'L0_ffn_fc2_w',
        'L0_ffn_fc2_b', 'L0_ffn_alpha']


def kernel(**inputs):
    import numpy as _np
    import concourse.bacc as _bacc
    from concourse import mybir as _mybir
    from concourse.bass_utils import run_bass_kernel_spmd as _run

    nc = _bacc.Bacc("TRN2", target_bir_lowering=False, num_devices=1)
    arrays, args = {}, []
    for name in _INS:
        a = _np.ascontiguousarray(inputs[name])
        arrays[f"in_{name}_dram"] = a
        args.append(nc.dram_tensor(f"in_{name}_dram", a.shape, _mybir.dt.from_np(a.dtype), kind="ExternalInput").ap())
    shape = inputs['x'].shape
    tokens = shape[0] * shape[1]
    out = nc.dram_tensor("out_dram", [tokens + 128, shape[2]], _mybir.dt.float32, kind="ExternalOutput").ap()
    flamingo_block(nc, *args, out)
    r = _run(nc, [arrays], core_ids=[0])
    return r.results[0]["out_dram"][:tokens].reshape(shape)
```

```python
from contextlib import ExitStack

import concourse.bass as bass
from concourse import mybir

ALU = mybir.AluOpType
ACT = mybir.ActivationFunctionType
AX = mybir.AxisListType
F32 = mybir.dt.float32
F16 = mybir.dt.float16
I32 = mybir.dt.int32
U32 = mybir.dt.uint32

P = 128
X_SCALE = 16.0
W_SCALE = 128.0
C_SCALE = 16.0
H_SCALE = 16.0
MASKED = -1.0e30
EPS = 1e-5


class Count:

    def __init__(self):
        self.n = 0

    def up(self, by=1):
        self.n += by
        return self.n


def flamingo_block(nc, x, ctx_sets, token_sets, g_xattn, g_ffn, desc, w_q, b_q, gate_w, gate_b,
                   fc1_w, fc1_b, fc2_w, fc2_b, alpha, out):
    B, S, D = x.shape
    NS = ctx_sets.shape[1]
    KSET = token_sets.shape[1]
    E, _, F = fc1_w.shape
    T = B * S
    NT = T // P
    GT = 4
    NG = NT // GT
    KC = D // P
    FC = F // P
    HALVES = S // P
    CAP = T + P
    TILES = (2 * T - E) // P + E
    SPARE = TILES - 2 * T // P
    W_COMB = D
    W_TOK = W_COMB + E
    ROW = W_TOK + 1
    NU = 2 * E
    NSTAGE = 4
    NX = 4
    HEAD = 8
    UNROLL = 4
    LOOPS = (TILES - HEAD) // UNROLL
    assert KC == 2 and HALVES == 2 and D == 256 and NG == 4 and FC == 8 and TILES == 39

    xt = x.rearrange("b (h p) d -> p (b h) d", p=P)
    out_t = out[0:T, :].rearrange("(t p) d -> p t d", p=P)
    xsort = nc.dram_tensor("xsort", [E * CAP + SPARE * P, ROW], I32, kind="Internal").ap()

    with ExitStack() as stack:
        def sb(name, shape, dt=F32):
            return stack.enter_context(nc.sbuf_tensor(name, shape, dt))

        def sem(name):
            return stack.enter_context(nc.semaphore(name))

        w1hi = sb("w1hi", [P, E, KC, F], F16)
        w1lo = sb("w1lo", [P, E, KC, F], F16)
        w2hi = sb("w2hi", [P, E, FC, D], F16)
        w2lo = sb("w2lo", [P, E, FC, D], F16)
        wstage = sb("wstage", [P, 2, KC * F])
        stage_buf = [wstage[:, 0, :], wstage[:, 1, :],
                     w1hi[:, E - 2:E].rearrange("p e k f -> p (e k f)").bitcast(F32),
                     w2hi[:, E - 2:E].rearrange("p e f d -> p (e f d)").bitcast(F32)]
        arena = sb("arena", [P, NT, D])
        xs = arena
        xn = sb("xn", [P, GT, D])
        xn1 = w2lo[:, E - 1].rearrange("p f d -> p (f d)").bitcast(F32).rearrange("p (t d) -> p t d", t=GT)
        xnT = sb("xnT", [P, 2, 2, KC, P])
        rows = sb("rows", [P, 2, GT, ROW], I32)
        stage_buf.append(rows[:, :, :, :].rearrange("p g t w -> p (g t w)")[:, 0:KC * F].bitcast(F32))
        early = rows[:, :, :, :].rearrange("p g t w -> p (g t w)").bitcast(F32)
        wq_sb = early[:, 0:2 * D].rearrange("p (c d) -> p c d", c=KC)
        bq_bc = early[:, 2 * D:3 * D].rearrange("p (c q) -> p c q", c=KC)
        desc_sb = early[0:NS, 3 * D:4 * D]
        bias_rows = early[0:E * FC + KC, 4 * D:4 * D + P]
        ctx_buf = sb("ctx_buf", [P, B, D])
        ctx_hi = w1lo[:, E - 2].rearrange("p k f -> p (k f)")
        ctx_lo = w1lo[0:NS, E - 1].rearrange("p k f -> p (k f)")
        descT = sb("descT", [P, KC, NS])
        proj = sb("proj", [P, KC, NS])
        itok = sb("itok", [P, HALVES, KSET], I32)
        itok_f = sb("itok_f", [P, HALVES, KSET])
        maskbias = sb("maskbias", [P, HALVES, NS])
        gcol = sb("gcol", [P, 2])
        tg = sb("tg", [P, 2])
        tg_gelu = sb("tg_gelu", [P, 2])
        gw_sb = sb("gw_sb", [P, KC, E])
        gb_bc = sb("gb_bc", [P, E])
        alpha_bc = sb("alpha_bc", [P, E])
        Q = P // 4
        b2_sb = sb("b2_sb", [2 * Q + E, D])
        b2_split = sb("b2_split", [3 * Q, D], F16)
        bias_cols = sb("bias_cols", [P, E * FC + KC])
        b1T = bias_cols[:, 0:E * FC].rearrange("p (e f) -> p e f", e=E)
        bq_col = bias_cols[:, E * FC:E * FC + KC]
        ident = sb("ident", [P, P])
        ident16 = sb("ident16", [P, P], F16)
        ones = sb("ones", [P, P])
        before = sb("before", [P, P])
        iota_i = sb("iota_i", [P, NS], I32)
        iota64 = sb("iota64", [P, NS])
        iota_h = sb("iota_h", [P, NS], F16)
        iota_ti = sb("iota_ti", [1, TILES], I32)
        iota_t = sb("iota_t", [1, TILES])
        region = sb("region", [P, E])
        pad_row = sb("pad_row", [P, ROW], I32)
        stats = sb("stats", [P, NT, 6])
        neg_half = sb("neg_half", [P, GT])
        mv1 = sb("mv1", [P, NT, 2])
        rstd1 = sb("rstd1", [P, NT])
        shift1 = sb("shift1", [P, NT])
        mv2 = sb("mv2", [P, NT, 2])
        rstd2 = sb("rstd2", [P, NT])
        shift2 = sb("shift2", [P, NT])
        masked = sb("masked", [P, GT, NS])
        top8 = sb("top8", [P, 2, GT, 8])
        top8i = sb("top8i", [P, 2, GT, 8], U32)
        top2h = sb("top2h", [P, 2, GT], F16)
        scale_a = sb("scale_a", [P, 2, GT])
        diff = sb("diff", [P, 2, GT])
        ediff = sb("ediff", [P, 2, GT])
        den = sb("den", [P, GT])
        wset = sb("wset", [P, 2, GT, NS])
        second = wset[:, 0, 0:GT // 2, :].rearrange("p t n -> p (t n)").bitcast(F16).rearrange("p (t n) -> p t n", n=NS)
        is_set = wset[:, 1, :, :].rearrange("p t n -> p (t n)").bitcast(F16).rearrange("p (k n) -> p k n", n=NS)
        wsum = sb("wsum", [P, GT, 2, NS], F16)
        wT_buf = sb("wT_buf", [P, GT * P])
        wT = wT_buf[:, 0:GT * P // 2].bitcast(F16).rearrange("p (t q) -> p t q", t=GT)
        e_hi = sb("e_hi", [P, 2, GT], F16)
        e_lo = sb("e_lo", [P, GT], F16)
        logit = sb("logit", [P, GT, E])
        gtop = sb("gtop", [P, 2, GT, 8])
        gtopi = sb("gtopi", [P, 2, GT, 8], U32)
        gtop2f = sb("gtop2f", [P, GT, 2])
        gdiff = sb("gdiff", [P, 2, GT])
        gediff = sb("gediff", [P, 2, GT])
        gden = sb("gden", [P, GT])
        gpair = sb("gpair", [P, GT, 2])
        onehot = sb("onehot", [P, GT, 2, E])
        oh_tmp = sb("oh_tmp", [P, GT, 2, E])
        comb = sb("comb", [P, 2, GT, E])
        comb_split = sb("comb_split", [P, 2, GT, 3, Q], F16)
        combT = sb("combT", [3 * Q, GT, P], F16)
        picks = sb("picks", [P, NT, E])
        earlier = sb("earlier", [P, NT + 1, E])
        slot_f = sb("slot_f", [P, GT, 2])
        slot_i = sb("slot_i", [P, NG, GT, 2], U32)
        cnt = sb("cnt", [P, E])
        cnt_i = sb("cnt_i", [P, E], I32)
        tl_i = sb("tl_i", [P, E], I32)
        tl = sb("tl", [P, E])
        ctl = sb("ctl", [P, E])
        pad_at = sb("pad_at", [1, E], I32)
        over = wset[0:1, :, :, :].rearrange("a k t n -> a (k t n)")[:, 0:TILES * E].rearrange("a (i e) -> a i e", e=E)
        over2 = wT_buf[0:1, 0:TILES * E].rearrange("a (i e) -> a i e", e=E)
        te_f = sb("te_f", [1, TILES])
        tc_f = sb("tc_f", [1, TILES])
        tr_f = sb("tr_f", [1, TILES])
        te_i = sb("te_i", [1, TILES], I32)
        tr_i = sb("tr_i", [1, TILES], I32)
        xg = ctx_buf[:, :, :].rearrange("p b d -> p (b d)")[:, 0:NX * ROW].bitcast(I32).rearrange(
            "p (s w) -> p s w", s=NX)
        b1cur = sb("b1cur", [P, NX, FC])
        wcur = sb("wcur", [P, NX])
        tokcur = sb("tokcur", [P, NX], U32)
        xT = xnT[:, 0, :, :, :].rearrange("p t k q -> p (t k q)").bitcast(F16).rearrange(
            "p (s a k q) -> p s a k q", s=2, a=2, k=KC)
        y_sb = xn[:, 0:2, :]
        flat = arena[:, :, :].rearrange("p t d -> p (t d)")
        h32 = [flat[:, j * F:(j + 1) * F] for j in range(2)]
        hhi = [flat[:, 2 * F + j * F // 2:2 * F + (j + 1) * F // 2].bitcast(F16) for j in range(2)]
        hlo = [flat[:, 3 * F + j * F // 2:3 * F + (j + 1) * F // 2].bitcast(F16) for j in range(2)]

        bank = [stack.enter_context(nc.psum_tensor(f"bank{i}", [P, 512], F32)) for i in range(8)]

        x_in = [sem(f"x_in{g}") for g in range(NG)]
        small_in = sem("small_in")
        small2_in = sem("small2_in")
        ctx_in = sem("ctx_in")
        ctx_hi_ready = sem("ctx_hi_ready")
        ctx_ready = sem("ctx_ready")
        b2_zero = sem("b2_zero")
        b2_hi_ready = sem("b2_hi_ready")
        b2_ready = sem("b2_ready")
        comb_split_ready = sem("comb_split_ready")
        w_in = [sem(f"w_in{s}") for s in range(NSTAGE + 1)]
        w_hi = sem("w_hi")
        w_lo = sem("w_lo")
        pool_const = sem("pool_const")
        pool_step = sem("pool_step")
        vec_step = sem("vec_step")
        gates_ready = sem("gates_ready")
        descT_ps = sem("descT_ps")
        descT_sb = sem("descT_sb")
        bq_ready = sem("bq_ready")
        proj_ps = sem("proj_ps")
        proj_ready = sem("proj_ready")
        bias_ps = sem("bias_ps")
        bias_read = sem("bias_read")
        stats1 = sem("stats1")
        stats2 = sem("stats2")
        ln1 = sem("ln1")
        xn1_done = sem("xn1_done")
        tr1_ps = sem("tr1_ps")
        pair_used = sem("pair_used")
        tr_pairs = sem("tr_pairs")
        scores_read = sem("scores_read")
        diff_ready = sem("diff_ready")
        exp_ready = sem("exp_ready")
        wset_ready = sem("wset_ready")
        wT_ps = sem("wT_ps")
        wT_sb = sem("wT_sb")
        attn_ps = sem("attn_ps")
        x1_ready = sem("x1_ready")
        ln2 = sem("ln2")
        xn2_done = sem("xn2_done")
        tr2_ps = sem("tr2_ps")
        hi_ready = sem("hi_ready")
        row_ready = sem("row_ready")
        last_row_ready = sem("last_row_ready")
        tokens_ready = sem("tokens_ready")
        gdiff_ready = sem("gdiff_ready")
        gexp_ready = sem("gexp_ready")
        comb_ready = sem("comb_ready")
        picks_ready = sem("picks_ready")
        rank_ps = sem("rank_ps")
        rank_read = sem("rank_read")
        slots_ready = sem("slots_ready")
        combT_ps = sem("combT_ps")
        combT_sb = sem("combT_sb")
        b2_ps = sem("b2_ps")
        init_ready = sem("init_ready")
        out_init = sem("out_init")
        pad_out_init = sem("pad_out_init")
        scattered = [sem(f"scattered{r}") for r in range(2)]
        count_ps = sem("count_ps")
        pads_ready = sem("pads_ready")
        spare_out = sem("spare_out")
        pads_out = sem("pads_out")
        table_ready = sem("table_ready")
        b1T_ps = sem("b1T_ps")
        b1T_sb = sem("b1T_sb")
        xg_in = [sem(f"xg_in{s}") for s in range(NX)]
        b1_ready = sem("b1_ready")
        cur_ready = sem("cur_ready")
        xT_ps = sem("xT_ps")
        xT_sb = sem("xT_sb")
        fc1_ps = sem("fc1_ps")
        gelu_done = sem("gelu_done")
        hi_done = sem("hi_done")
        lo_done = sem("lo_done")
        y_ps = sem("y_ps")
        y_ready = sem("y_ready")
        add_started = sem("add_started")
        added = sem("added")

        NSMALL, NSMALL2 = 5, 8
        xn2_of = [xn] * (NG - 1) + [xn1]

        def unit_parts(u):
            e = u // 2
            if u % 2 == 0:
                return w1hi[:, e].rearrange("p k f -> p (k f)"), w1lo[:, e].rearrange("p k f -> p (k f)")
            return w2hi[:, e].rearrange("p k f -> p (k f)"), w2lo[:, e].rearrange("p k f -> p (k f)")

        STEPS = NG + 3
        UNITS = [1, 1, 1, 2, 2, 1, 2]
        LATE = [1, 1, 1, 1, 1, 1, 0, 0]
        LO_FIRST = [0, 1, 1, 1, 1, 1, 0]
        LO_AFTER = [0, 0, 0, 0, 1, 1, 2]
        lo_at = [sum(LO_FIRST[:s]) + sum(LO_AFTER[:s]) for s in range(STEPS + 1)]
        unit_at = [sum(UNITS[:s]) for s in range(STEPS + 1)]
        late_at = [unit_at[-1] + sum(LATE[:i]) for i in range(HEAD + 1)]
        assert late_at[HEAD - 1] == NU and all(late_at[max(i - 1, 0)] >= min(2 * (i + 1), NU) for i in range(HEAD))

        stage_of = [u % NSTAGE if u < NU - 4 else (0, 1, NSTAGE, 0)[u - NU + 4] for u in range(NU)]
        before_in = [max([w for w in range(u) if stage_of[w] == stage_of[u]], default=None) for u in range(NU)]
        nth_in = [stage_of[:u + 1].count(stage_of[u]) for u in range(NU)]

        pair_at = {(1, 0): 0}
        for s in range(STEPS):
            if 0 <= s - 2 < NG:
                pair_at[(2, s - 2)] = 2 * len(pair_at)
            if s + 1 < NG:
                pair_at[(1, s + 1)] = 2 * len(pair_at)

        block = stack.enter_context(nc.Block())

        @block.sync
        def _(sp):
            def load_unit(u):
                e, s = u // 2, stage_of[u]
                if before_in[u] is not None:
                    sp.wait_ge(w_hi, before_in[u] + 1)
                    sp.wait_ge(w_lo, before_in[u] + 1)
                if u % 2 == 0:
                    src = fc1_w[e].rearrange("(k p) f -> p k f", p=P)
                    dst = stage_buf[s].rearrange("p (k f) -> p k f", k=KC)
                else:
                    src = fc2_w[e].rearrange("(k p) d -> p k d", p=P)
                    dst = stage_buf[s].rearrange("p (k d) -> p k d", k=FC)
                sp.dma_start(dst, src).then_inc(w_in[s], 16)

            def load_tokens(g):
                sp.dma_start(xs[:, g * GT:(g + 1) * GT, :], xt[:, g * GT:(g + 1) * GT, :]).then_inc(x_in[g], 16)

            load_tokens(0)
            for dst, src in (
                (gcol[:, 0:1], g_xattn.rearrange("(a b) -> a b", a=1).to_broadcast([P, 1])),
                (gcol[:, 1:2], g_ffn.rearrange("(a b) -> a b", a=1).to_broadcast([P, 1])),
                (gw_sb[:, :, :], gate_w.rearrange("(c p) e -> p c e", p=P)),
                (gb_bc[:, :], gate_b.rearrange("(a e) -> a e", a=1).to_broadcast([P, E])),
                (alpha_bc[:, :], alpha.rearrange("(a e) -> a e", a=1).to_broadcast([P, E])),
                (b2_sb[0:E, :], fc2_b[:, :]),
                (b2_sb[Q:Q + E, :], fc2_b[:, :]),
                (b2_sb[2 * Q:2 * Q + E, :], fc2_b[:, :]),
            ):
                sp.dma_start(dst, src).then_inc(small2_in, 16)
            load_tokens(1)
            for h in range(2):
                sp.dma_start(ctx_buf[h * NS:(h + 1) * NS, :, :], ctx_sets.rearrange("b n d -> n b d")).then_inc(ctx_in, 16)
            load_tokens(2)
            load_tokens(3)
            sp.wait_ge(small_in, 16 * NSMALL)
            sp.wait_ge(small2_in, 16 * NSMALL2)
            for u in range(NSTAGE):
                load_unit(u)
            sp.wait_ge(pool_const, 3)
            for k in range(SPARE):
                sp.dma_start(xsort[E * CAP + k * P:E * CAP + (k + 1) * P, :], pad_row[:, :]).then_inc(spare_out, 16)
            sp.dma_start(out[T:T + P, :], pad_row[:, 0:D].bitcast(F32)).then_inc(pad_out_init, 16)
            for u in range(NSTAGE, unit_at[-1]):
                load_unit(u)
            sp.wait_ge(pads_ready, 1)
            pad_rows = nc.values_load_multi_w_load_instructions(
                pad_at[0:1, 0:E], engines=[mybir.EngineType.SP], min_val=0, max_val=(E - 1) * CAP + T,
                skip_runtime_bounds_check_because="an expert has at most T rows from the start of its region")[1]
            for at in pad_rows:
                sp.dma_start(xsort[bass.ds(at, P), :], pad_row[:, :]).then_inc(pads_out, 16)

            def first_row(i):
                return sp.value_load(tr_i[0:1, bass.ds(i, 1)], min_val=0, max_val=E * CAP + (SPARE - 1) * P)

            def load_tile(i, s, row=None):
                row = first_row(i) if row is None else row
                sp.dma_start(xg[:, s, :], xsort[bass.ds(row, P), :]).then_inc(xg_in[s], 16)

            sp.wait_ge(table_ready, 1)
            first_rows = [first_row(i) for i in range(NX)]
            for r in range(2):
                sp.wait_ge(scattered[r], 16 * 4 * GT)
            sp.wait_ge(spare_out, 16 * SPARE)
            sp.wait_ge(pads_out, 16 * E)
            for i in range(NX):
                load_tile(i, i, first_rows[i])
            u = unit_at[-1]
            while (before_in[u] or 0) < unit_at[-1]:
                load_unit(u)
                u += 1
            for i in range(NX, HEAD + NX):
                sp.wait_ge(cur_ready, i - NX + 1)
                load_tile(i, i % NX)
                while u < NU and (before_in[u] or 0) < late_at[i - NX + 1]:
                    load_unit(u)
                    u += 1
            assert u == NU
            with sp.Fori(HEAD // NX + 1, TILES // NX) as m:
                for s in range(NX):
                    sp.wait_ge(cur_ready, m * NX + (s + 1 - NX))
                    load_tile(m * NX + s, s)
            for i in range(TILES // NX * NX, TILES):
                sp.wait_ge(cur_ready, i - NX + 1)
                load_tile(i, i % NX)

        @block.tensor
        def _(pe):
            pe.wait_ge(small_in, 16 * NSMALL)
            pe.wait_ge(pool_const, 1)
            for c in range(KC):
                mm = pe.transpose(bank[2][:, c * NS:(c + 1) * NS], desc_sb[:, c * P:(c + 1) * P], ident[0:NS, 0:NS])
            mm.then_inc(descT_ps, 1)
            nb = E * FC + KC
            pe.transpose(bank[4][:, 0:nb], bias_rows[:, :], ident[0:nb, 0:nb]).then_inc(b1T_ps, 1)
            pe.wait_ge(descT_sb, 1)
            for k in range(KC):
                for c in range(KC):
                    mm = pe.matmul(bank[3][:, k * NS:(k + 1) * NS], wq_sb[:, c, k * P:(k + 1) * P], descT[:, c, :],
                                   start=(c == 0), stop=(c == KC - 1))
            mm.then_inc(proj_ps, 1)
            pe.wait_ge(bq_ready, 1)
            for c in range(KC):
                mm = pe.matmul(bank[4][:, 2 * NS:3 * NS], bq_bc[:, c, :], descT[:, c, :],
                               start=(c == 0), stop=(c == KC - 1))
            mm.then_inc(bias_ps, 1)

            def transpose_pairs(ln, g, rows_in, done_sem, ps_sem):
                base = pair_at[(ln, g)]
                for j in range(2):
                    pe.wait_ge(done_sem, g * GT + 2 * j + 2)
                    if base + j >= 2:
                        pe.wait_ge(tr_pairs, base + j - 1)
                    for t in range(2):
                        for k in range(KC):
                            mm = pe.transpose(bank[(base + j) % 2][:, (t * KC + k) * P:(t * KC + k + 1) * P],
                                              rows_in[:, 2 * j + t, k * P:(k + 1) * P], ident[:, :])
                    mm.then_inc(ps_sem, 1)

            def multiply_pairs(ln, g, rhs, n, put):
                base = pair_at[(ln, g)]
                if ln == 1 and g == 0:
                    pe.wait_ge(proj_ready, 1)
                if ln == 2 and g >= 1:
                    pe.wait_ge(rank_read, g)
                for j in range(2):
                    pe.wait_ge(tr_pairs, base + j + 1)
                    for t in range(2):
                        q = 2 * j + t
                        for k in range(KC):
                            mm = pe.matmul(put[:, q * n:(q + 1) * n], xnT[:, (base + j) % 2, t, k, :], rhs[:, k, :],
                                           start=(k == 0), stop=(k == KC - 1))
                    mm.then_inc(pair_used, 1)

            def scores(g):
                if g >= 2:
                    pe.wait_ge(scores_read, g - 1)
                transpose_pairs(1, g, xn1, xn1_done, tr1_ps)
                multiply_pairs(1, g, proj, NS, bank[2 + g % 2])

            def attention(g):
                pe.wait_ge(wset_ready, g + 1)
                if g == 0:
                    pe.wait_ge(bias_read, HALVES)
                if g >= 3:
                    pe.wait_ge(combT_sb, g - 2)
                tb = bank[4][:, 0:GT * P // 2].bitcast(F16)
                for t in range(GT):
                    mm = pe.transpose(tb[:, t * P:(t + 1) * P], wsum[:, t, :, :].rearrange("p a n -> p (a n)"), ident16[:, :])
                mm.then_inc(wT_ps, 1)
                pe.wait_ge(wT_sb, g + 1)
                if g == 0:
                    pe.wait_ge(ctx_ready, 1)
                for j in range(2):
                    if g == 1:
                        pe.wait_ge(x1_ready, j + 1)
                    if g == 2:
                        pe.wait_ge(x1_ready, 2 + j + 1)
                    if g >= 3:
                        pe.wait_ge(init_ready, 2 * (g - 3) + j + 1)
                    for t in range(2):
                        q = 2 * j + t
                        put = bank[5 + j][:, t * D:(t + 1) * D]
                        b = (g * GT + q) // HALVES
                        pe.matmul(put, wT[:, q, :], ctx_hi[:, b * D:(b + 1) * D], start=True, stop=False)
                        mm = pe.matmul(put, wT[0:NS, q, :], ctx_lo[:, b * D:(b + 1) * D], start=False, stop=True)
                    mm.then_inc(attn_ps, 1)

            def logits(g):
                if g == 0:
                    pe.wait_ge(small2_in, 16 * NSMALL2)
                multiply_pairs(2, g, gw_sb, E, bank[7])

            def ranks(g):
                pe.wait_ge(picks_ready, g + 1)
                if g == NG - 1:
                    pe.matmul(bank[7][:, GT * E:(GT + 1) * E], ones[:, :], earlier[:, NT, :],
                              start=True, stop=True).then_inc(count_ps, 1)
                tiles = slice(g * GT, (g + 1) * GT)
                pe.matmul(bank[7][:, 0:GT * E], before[:, :], picks[:, tiles, :].rearrange("p t e -> p (t e)"),
                          start=True, stop=False)
                pe.matmul(bank[7][:, 0:GT * E], ones[:, :], earlier[:, tiles, :].rearrange("p t e -> p (t e)"),
                          start=False, stop=True).then_inc(rank_ps, 1)

            def bias2(g):
                pe.wait_ge(comb_split_ready, g + 1)
                if g == 0:
                    pe.wait_ge(b2_ready, 1)
                pe.wait_ge(wT_sb, min(g + 3, NG))
                for t in range(GT):
                    mm = pe.transpose(bank[4][0:3 * Q, 0:GT * P // 2].bitcast(F16)[:, t * P:(t + 1) * P],
                                      comb_split[:, g % 2, t, :, :].rearrange("p a e -> p (a e)"), ident16[:, :])
                mm.then_inc(combT_ps, 1)
                pe.wait_ge(combT_sb, g + 1)
                for j in range(2):
                    pe.wait_ge(x1_ready, 2 * min(g + 2, NG - 1) + j + 1)
                    if g + 2 >= NG:
                        pe.wait_ge(init_ready, 2 * (g - 1) + j + 1)
                    for t in range(2):
                        mm = pe.matmul(bank[5 + j][:, t * D:(t + 1) * D], combT[:, 2 * j + t, :], b2_split[:, :],
                                       start=True, stop=True)
                    mm.then_inc(b2_ps, 1)

            scores(0)
            for s in range(STEPS):
                if 0 <= s - 1 < NG:
                    attention(s - 1)
                if 0 <= s - 2 < NG - 1:
                    transpose_pairs(2, s - 2, xn, xn2_done, tr2_ps)
                    logits(s - 2)
                if s + 1 < NG:
                    scores(s + 1)
                if s == NG + 1:
                    ranks(NG - 1)
                if 0 <= s - 3 < NG:
                    bias2(s - 3)
                if s == NG:
                    transpose_pairs(2, NG - 1, xn1, xn2_done, tr2_ps)
                if 0 <= s - 2 < NG - 1:
                    ranks(s - 2)
                if s == NG:
                    logits(NG - 1)

            def transpose_tile(i, s):
                pe.wait_ge(xg_in[s % NX], i // NX * 16 + 16 if isinstance(i, int) else (i - s % NX) * (16 // NX) + 16)
                if not (isinstance(i, int) and i < 2):
                    pe.wait_ge(xT_sb, i - 1)
                part = xg[:, s % NX, 0:D].bitcast(F16)
                tb = bank[6 + s % 2][:, 0:D].bitcast(F16)
                for q in range(2 * KC):
                    mm = pe.transpose(tb[:, q * P:(q + 1) * P], part[:, q * P:(q + 1) * P], ident16[:, :])
                mm.then_inc(xT_ps, 1)

            def fc1_operands(c, e):
                return [[w[:, bass.ds(e, 1), k, c * P:(c + 1) * P].rearrange("p a f -> p (a f)")
                         for w in (w1hi, w1lo)] for k in range(KC)]

            def fc2_operands(c, e):
                return [w[:, bass.ds(e, 1), c, :].rearrange("p a d -> p (a d)") for w in (w2hi, w2lo)]

            def fc1(i, s, c, ws):
                half = c // (FC // 2)
                if c == 0:
                    pe.wait_ge(xT_sb, i + 1)
                if c % (FC // 2) == 0 and not (isinstance(i, int) and i < 2):
                    pe.wait_ge(gelu_done, i * 2 + (half - 3))
                put = bank[2 * (s % 2) + half][:, c % (FC // 2) * P:(c % (FC // 2) + 1) * P]
                for k in range(KC):
                    hi, lo = ws[k]
                    for n, (w, x_part) in enumerate(((hi, 0), (hi, 1), (lo, 0))):
                        mm = pe.matmul(put, w, xT[:, s % 2, x_part, k, :],
                                       start=(k == 0 and n == 0), stop=(k == KC - 1 and n == 2))
                if c % (FC // 2) == FC // 2 - 1:
                    mm.then_inc(fc1_ps, 1)

            def fc2(i, s, c, ws):
                yb = bank[4 + s % 2][:, 0:D]
                if c == 0 and not (isinstance(i, int) and i < 2):
                    pe.wait_ge(y_ready, i - 1)
                if c % (FC // 2) == 0:
                    pe.wait_ge(lo_done, i * 2 + (c // (FC // 2) + 1))
                hp = hhi[s % 2][:, c * P:(c + 1) * P]
                lp = hlo[s % 2][:, c * P:(c + 1) * P]
                for n, (h, w) in enumerate(((hp, ws[0]), (hp, ws[1]), (lp, ws[0]))):
                    mm = pe.matmul(yb, h, w, start=(c == 0 and n == 0), stop=(c == FC - 1 and n == 2))
                if c == FC - 1:
                    mm.then_inc(y_ps, 1)

            def experts(i, n):
                return nc.values_load_multi_w_load_instructions(
                    te_i[0:1, bass.ds(i, n)], engines=[mybir.EngineType.PE], min_val=0, max_val=E - 1,
                    skip_runtime_bounds_check_because="table() keeps the experts within 0 .. E - 1")[1]

            def tile(i, s, e, e1, e2, nxt=True):
                for c in range(FC):
                    back, e_b, c_b = (2, e2, c + FC // 2) if c < FC // 2 else (1, e1, c - FC // 2)
                    w1 = fc1_operands(c, e) if e is not None else None
                    w2 = fc2_operands(c_b, e_b) if e_b is not None else None
                    if w1:
                        for k in range(KC):
                            for w in w1[k]:
                                pe.lower_ap(w, for_matmul_weights=True)
                    if w2:
                        for w in w2:
                            pe.lower_ap(w)
                    if w1:
                        fc1(i, s, c, w1)
                    if w2:
                        fc2(i - back, s + NX - back, c_b, w2)
                    if c == 2 and nxt:
                        transpose_tile(i + 1, s + 1)

            pe.wait_ge(table_ready, 1)
            pe.wait_ge(b2_ps, 2 * NG)
            pe.wait_ge(init_ready, 2 * NG)
            transpose_tile(0, 0)
            es = [None, None, *experts(0, HEAD)]
            for i in range(HEAD):
                pe.wait_ge(w_hi, 2 * (i + 1))
                pe.wait_ge(w_lo, 2 * (i + 1))
                tile(i, i % NX, es[i + 2], es[i + 1], es[i])
            with pe.Fori(0, LOOPS) as m:
                es = experts(m * UNROLL + (HEAD - 2), UNROLL + 2)
                for s in range(UNROLL):
                    tile(m * UNROLL + (HEAD + s), s % NX, es[s + 2], es[s + 1], es[s])
            tail = HEAD + LOOPS * UNROLL
            es = [*experts(tail - 2, TILES - tail + 2), None, None]
            for i in range(tail, TILES + 2):
                tile(i, i % NX, es[i - tail + 2], es[i - tail + 1], es[i - tail], nxt=(i < TILES - 1))

        @block.scalar
        def _(act):
            for dst, src in (
                (desc_sb[:, :], desc[:, :]),
                (wq_sb[:, :, :], w_q.rearrange("(c p) d -> p c d", p=P)),
                (bias_rows[E * FC:E * FC + KC, :], b_q.rearrange("(c p) -> c p", p=P)),
                (bias_rows[0:E * FC, :], fc1_b.rearrange("e (f p) -> (e f) p", p=P)),
                (itok[:, :, :], token_sets.rearrange("(h p) k -> p h k", p=P)),
            ):
                act.dma_start(dst, src).then_inc(small_in, 16)

            def normalise(g, dst, rstd, shift, done_sem):
                for t in range(GT):
                    n = g * GT + t
                    act.activation(dst[:, t, :], xs[:, n, :], ACT.Identity, bias=shift[:, n:n + 1],
                                   scale=rstd[:, n:n + 1]).then_inc(done_sem, 1)

            def copy_pairs(ln, g, ps_sem, pairs=(0, 1)):
                for j in pairs:
                    u = pair_at[(ln, g)] + j
                    act.wait_ge(ps_sem, 2 * g + j + 1)
                    if u >= 2:
                        act.wait_ge(pair_used, u - 1)
                    act.activation(xnT[:, u % 2, :, :, :].rearrange("p t k q -> p (t k q)"), bank[u % 2][:, :],
                                   ACT.Copy).then_inc(tr_pairs, 1)

            def norm1(g):
                act.wait_ge(ln1, g + 1)
                if g >= 1:
                    act.wait_ge(tr1_ps, 2 * g)
                normalise(g, xn1, rstd1, shift1, xn1_done)

            def norm2(g):
                act.wait_ge(ln2, g + 1)
                if g == NG - 1:
                    act.wait_ge(tr1_ps, 2 * NG)
                elif g >= 1:
                    act.wait_ge(tr2_ps, 2 * g)
                    act.wait_ge(row_ready, g)
                normalise(g, xn2_of[g], rstd2, shift2, xn2_done)

            def rows_hi(g):
                act.wait_ge(xn2_done, (g + 1) * GT)
                if g >= 2:
                    act.wait_ge(scattered[g % 2], 16 * 2 * GT)
                act.activation(rows[:, g % 2, :, 0:P].bitcast(F16), xn2_of[g][:, :, :], ACT.Copy).then_inc(hi_ready, 1)

            def weights_hi(u):
                act.wait_ge(w_in[stage_of[u]], 16 * nth_in[u])
                if u == NU - 4:
                    act.wait_ge(w_lo, u)
                act.activation(unit_parts(u)[0], stage_buf[stage_of[u]], ACT.Copy, scale=W_SCALE).then_inc(w_hi, 1)

            def route_exp(g):
                act.wait_ge(gdiff_ready, g + 1)
                act.activation(gediff[:, g % 2, :], gdiff[:, g % 2, :], ACT.Exp).then_inc(gexp_ready, 1)

            def store_rows(g):
                act.wait_ge(init_ready, 2 * (g + 1))
                act.dma_start(out_t[:, g * GT:(g + 1) * GT, :], xs[:, g * GT:(g + 1) * GT, :]).then_inc(out_init, 16)

            norm1(0)
            copy_pairs(1, 0, tr1_ps)
            act.wait_ge(small2_in, 16 * NSMALL2)
            act.activation(tg[:, :], gcol[:, :], ACT.Tanh).then_inc(gates_ready, 1)
            norm1(1)
            for s in range(STEPS):
                if s < NG:
                    act.wait_ge(diff_ready, s + 1)
                    act.activation(ediff[:, s % 2, :], diff[:, s % 2, :], ACT.Exp)
                    act.activation(e_hi[:, s % 2, :], diff[:, s % 2, :], ACT.Exp).then_inc(exp_ready, 1)
                if s == 0:
                    copy_pairs(1, 1, tr1_ps)
                    act.wait_ge(ctx_in, 16 * 2)
                    act.activation(ctx_hi, ctx_buf[:, :, :].rearrange("p b d -> p (b d)"), ACT.Copy,
                                   scale=C_SCALE).then_inc(ctx_hi_ready, 1)
                    act.wait_ge(b2_zero, 1)
                    for q in range(3):
                        op = act.activation(b2_split[q * Q:q * Q + E, :], b2_sb[q * Q:q * Q + E, :], ACT.Copy,
                                            scale=W_SCALE)
                    op.then_inc(b2_hi_ready, 1)
                if 0 <= s - 1 < NG:
                    act.wait_ge(wT_ps, s)
                    act.activation(wT[:, :, :].rearrange("n t p -> n (t p)"), bank[4][:, 0:GT * P // 2].bitcast(F16),
                                   ACT.Copy).then_inc(wT_sb, 1)
                if 0 <= s - 2 < NG - 1:
                    norm2(s - 2)
                    copy_pairs(2, s - 2, tr2_ps)
                if 1 < s + 1 < NG:
                    norm1(s + 1)
                if 0 <= s - 2 < NG:
                    rows_hi(s - 2)
                if 1 < s + 1 < NG:
                    copy_pairs(1, s + 1, tr1_ps, pairs=(0,))
                if s == NG:
                    norm2(NG - 1)
                if 0 <= s - 2 < NG - 1:
                    route_exp(s - 2)
                if 1 < s + 1 < NG:
                    copy_pairs(1, s + 1, tr1_ps, pairs=(1,))
                if s == NG + 1:
                    route_exp(NG - 1)
                if 0 <= s - 3 < NG:
                    act.wait_ge(combT_ps, s - 2)
                    act.activation(combT[:, :, :].rearrange("e t p -> e (t p)"),
                                   bank[4][0:3 * Q, 0:GT * P // 2].bitcast(F16), ACT.Copy).then_inc(combT_sb, 1)
                if s == NG:
                    copy_pairs(2, NG - 1, tr2_ps)
                for u in range(unit_at[s], unit_at[s + 1]):
                    weights_hi(u)
                if 0 <= s - 4 < NG:
                    store_rows(s - 4)
            store_rows(NG - 1)
            act.activation(tg_gelu[:, :], gcol[:, :], ACT.Gelu)

            def gelu(i, s, half):
                if half == 0:
                    act.wait_ge(b1_ready, i + 1)
                act.wait_ge(fc1_ps, i * 2 + (half + 1))
                if not (isinstance(i, int) and i < 2):
                    act.wait_ge(lo_done, i * 2 + (half - 3))
                for c in range(FC // 2):
                    f = half * (FC // 2) + c
                    op = act.activation(h32[s % 2][:, f * P:(f + 1) * P],
                                        bank[2 * (s % 2) + half][:, c * P:(c + 1) * P], ACT.Gelu,
                                        bias=b1cur[:, s % NX, f:f + 1], scale=1.0 / (X_SCALE * W_SCALE))
                op.then_inc(gelu_done, 1)

            def weigh(i, s):
                act.wait_ge(cur_ready, i + 1)
                act.wait_ge(y_ps, i + 1)
                if not (isinstance(i, int) and i < 2):
                    act.wait_ge(added, i * 16 - 16)
                act.activation(y_sb[:, s % 2, :], bank[4 + s % 2][:, 0:D], ACT.Copy,
                               scale=wcur[:, s % NX:s % NX + 1]).then_inc(y_ready, 1)

            def tile(i, s, first=False):
                gelu(i, s, 0)
                if not first:
                    weigh(i - 2, s + NX - 2)
                gelu(i, s, 1)

            act.wait_ge(out_init, 16 * NG)
            for i in range(HEAD):
                tile(i, i % NX, first=(i < 2))
                for u in range(late_at[i], late_at[i + 1]):
                    weights_hi(u)
            with act.Fori(0, LOOPS) as m:
                for s in range(UNROLL):
                    tile(m * UNROLL + (HEAD + s), s % NX)
            for i in range(HEAD + LOOPS * UNROLL, TILES):
                tile(i, i % NX)
            for i in range(TILES - 2, TILES):
                weigh(i, i % NX)

        @block.vector
        def _(v):
            done = Count()

            def row_stats(g, tiles, mv, stats_done):
                for t in tiles:
                    v.bn_stats(stats[:, g * GT + t, :], xs[:, g * GT + t, :]).then_inc(vec_step, 1)
                v.wait_ge(vec_step, done.up(len(tiles)))
                for t in tiles:
                    v.bn_aggr(mv[:, g * GT + t, :], stats[:, g * GT + t, :]).then_inc(stats_done, 1)

            def norm1_stats(g):
                v.wait_ge(x_in[g], 16)
                row_stats(g, range(GT), mv1, stats1)

            v.memset(ones[:, :], 1.0).then_inc(vec_step, 1)
            v.memset(comb_split[:, :, :, :, :], 0.0)
            v.memset(b2_split[:, :], 0.0).then_inc(b2_zero, 1)
            v.memset(earlier[:, 0, :], 0.0).then_inc(vec_step, 1)
            v.wait_ge(vec_step, done.up(2))
            norm1_stats(0)
            v.wait_ge(small_in, 16 * NSMALL)
            v.wait_ge(pool_const, 3)
            v.wait_ge(descT_ps, 1)
            v.tensor_copy(descT[:, :, :].rearrange("p c n -> p (c n)"), bank[2][:, 0:KC * NS]).then_inc(descT_sb, 1)
            v.wait_ge(b1T_ps, 1)
            v.tensor_copy(bias_cols[:, :], bank[4][:, 0:E * FC + KC]).then_inc(b1T_sb, 1)
            v.wait_ge(b1T_sb, 1)
            for c in range(KC):
                op = v.tensor_scalar(bq_bc[:, c, :], ones[:, :], bq_col[:, c:c + 1], None, ALU.mult)
            op.then_inc(bq_ready, 1)
            norm1_stats(1)
            v.wait_ge(proj_ps, 1)
            v.tensor_copy(proj[:, :, :].rearrange("p c n -> p (c n)"), bank[3][:, 0:KC * NS]).then_inc(proj_ready, 1)
            v.tensor_copy(itok_f[:, :, :], itok[:, :, :]).then_inc(vec_step, 1)
            v.tensor_copy(iota64[:, :], iota_i[:, :]).then_inc(vec_step, 1)
            v.tensor_copy(iota_h[:, :], iota_i[:, :]).then_inc(vec_step, 1)
            v.tensor_copy(iota_t[:, :], iota_ti[:, :]).then_inc(vec_step, 1)
            v.tensor_copy(ident16[:, :], ident[:, :]).then_inc(vec_step, 1)
            v.wait_ge(vec_step, done.up(5))
            v.tensor_scalar(region[:, :], iota64[:, 0:E], float(CAP), None, ALU.mult).then_inc(vec_step, 1)
            v.tensor_scalar(earlier[0:1, 0, :], iota64[0:1, 0:E], float(CAP), None, ALU.mult).then_inc(vec_step, 1)
            for h in range(HALVES):
                v.tensor_scalar(maskbias[:, h, :], iota64[:, :], itok_f[:, h, 0:1], None, ALU.is_equal).then_inc(vec_step, 1)
            v.wait_ge(vec_step, done.up(4))
            for k in range(1, KSET):
                for h in range(HALVES):
                    v.scalar_tensor_tensor(out=maskbias[:, h, :], in0=iota64[:, :], scalar=itok_f[:, h, k:k + 1],
                                           in1=maskbias[:, h, :], op0=ALU.is_equal, op1=ALU.max).then_inc(vec_step, 1)
                v.wait_ge(vec_step, done.up(HALVES))
            v.tensor_scalar(maskbias[:, :, :], maskbias[:, :, :], -MASKED, MASKED, ALU.mult, ALU.add).then_inc(vec_step, 1)
            v.wait_ge(vec_step, done.up())
            v.wait_ge(bias_ps, 1)
            for h in range(HALVES):
                v.scalar_tensor_tensor(out=maskbias[:, h, :], in0=bank[4][:, 2 * NS:3 * NS], scalar=D ** -0.5,
                                       in1=maskbias[:, h, :], op0=ALU.mult, op1=ALU.add).then_inc(bias_read, 1)
            v.wait_ge(bias_read, HALVES)

            def pick_sets(g):
                v.wait_ge(pair_used, pair_at[(1, g)] + 2)
                v.scalar_tensor_tensor(
                    out=masked[:, :, :].rearrange("p (b h) n -> p b (h n)", h=HALVES),
                    in0=bank[2 + g % 2][:, 0:GT * NS].rearrange("p (b n) -> p b n", b=GT // HALVES), scalar=D ** -0.5,
                    in1=maskbias[:, :, :].rearrange("p h n -> p (h n)").unsqueeze(1).to_broadcast([P, GT // HALVES, HALVES * NS]),
                    op0=ALU.mult, op1=ALU.add).then_inc(scores_read, 1)
                v.wait_ge(scores_read, g + 1)
                for t in range(GT):
                    v.max(top8[:, g % 2, t, :], masked[:, t, :]).then_inc(vec_step, 1)
                v.wait_ge(vec_step, done.up(GT))
                v.tensor_tensor(diff[:, g % 2, :], top8[:, g % 2, :, 1], top8[:, g % 2, :, 0], ALU.subtract).then_inc(diff_ready, 1)
                for t in range(GT):
                    v.max_index(top8i[:, g % 2, t, :], top8[:, g % 2, t, :], masked[:, t, :]).then_inc(vec_step, 1)
                v.wait_ge(vec_step, done.up(GT))

            def set_weights(g):
                e2 = ediff[:, g % 2, :]
                v.tensor_copy(top2h[:, :, :], top8i[:, g % 2, :, 0:2].rearrange("p t k -> p k t")).then_inc(vec_step, 1)
                v.wait_ge(vec_step, done.up())
                v.tensor_tensor(is_set[:, :, :], iota_h[:, :].unsqueeze(1).to_broadcast([P, 2 * GT, NS]),
                                top2h[:, :, :].rearrange("p k t -> p (k t)").unsqueeze(2).to_broadcast([P, 2 * GT, NS]),
                                ALU.is_equal).then_inc(vec_step, 1)
                v.wait_ge(exp_ready, g + 1)
                if g == 0:
                    v.wait_ge(gates_ready, 1)
                    v.wait_ge(small2_in, 16 * NSMALL2)
                v.tensor_tensor(e_lo[:, :], e2, e_hi[:, g % 2, :], ALU.subtract).then_inc(vec_step, 1)
                v.tensor_scalar(den[:, :], e2, 1.0, None, ALU.add).then_inc(vec_step, 1)
                v.wait_ge(vec_step, done.up(3))
                if g >= 1:
                    v.wait_ge(wT_ps, g)
                is_second = is_set[:, GT:2 * GT, :]
                v.tensor_tensor(second[:, :, :], is_second, e_hi[:, g % 2, :].unsqueeze(2).to_broadcast([P, GT, NS]),
                                ALU.mult).then_inc(vec_step, 1)
                v.tensor_tensor(wsum[:, :, 1, :], is_second, e_lo[:, :].unsqueeze(2).to_broadcast([P, GT, NS]),
                                ALU.mult).then_inc(vec_step, 1)
                v.reciprocal(den[:, :], den[:, :]).then_inc(vec_step, 1)
                v.wait_ge(vec_step, done.up(3))
                v.tensor_tensor(wsum[:, :, 0, :], second[:, :, :], is_set[:, 0:GT, :], ALU.add).then_inc(wset_ready, 1)
                v.tensor_scalar(scale_a[:, g % 2, :], den[:, :], tg[:, 0:1], 1.0 / C_SCALE, ALU.mult, ALU.mult).then_inc(vec_step, 1)
                v.wait_ge(vec_step, done.up())
                v.wait_ge(wset_ready, g + 1)

            def add_attention(g):
                for j in range(2):
                    v.wait_ge(attn_ps, 2 * g + j + 1)
                    for t in range(2):
                        q = 2 * j + t
                        row = xs[:, g * GT + q, :]
                        op = v.scalar_tensor_tensor(out=row, in0=bank[5 + j][:, t * D:(t + 1) * D],
                                                    scalar=scale_a[:, g % 2, q:q + 1], in1=row,
                                                    op0=ALU.mult, op1=ALU.add)
                    op.then_inc(x1_ready, 1)
                    v.wait_ge(x1_ready, 2 * g + j + 1)
                    row_stats(g, range(2 * j, 2 * j + 2), mv2, stats2)

            def route(g):
                v.wait_ge(pair_used, pair_at[(2, g)] + 2)
                v.scalar_tensor_tensor(out=logit[:, :, :], in0=bank[7][:, 0:GT * E].rearrange("p (t e) -> p t e", t=GT),
                                       scalar=1.0 / X_SCALE, in1=gb_bc[:, :].unsqueeze(1).to_broadcast([P, GT, E]),
                                       op0=ALU.mult, op1=ALU.add).then_inc(vec_step, 1)
                v.wait_ge(vec_step, done.up())
                for t in range(GT):
                    v.max(gtop[:, g % 2, t, :], logit[:, t, :]).then_inc(vec_step, 1)
                v.wait_ge(vec_step, done.up(GT))
                v.tensor_tensor(gdiff[:, g % 2, :], gtop[:, g % 2, :, 1], gtop[:, g % 2, :, 0], ALU.subtract).then_inc(gdiff_ready, 1)
                for t in range(GT):
                    v.max_index(gtopi[:, g % 2, t, :], gtop[:, g % 2, t, :], logit[:, t, :]).then_inc(vec_step, 1)
                v.wait_ge(vec_step, done.up(GT))
                v.tensor_copy(gtop2f[:, :, :], gtopi[:, g % 2, :, 0:2]).then_inc(vec_step, 1)
                v.wait_ge(vec_step, done.up())
                v.tensor_tensor(onehot[:, :, :, :].rearrange("p t k e -> p (t k) e"),
                                iota64[:, 0:E].unsqueeze(1).to_broadcast([P, GT * 2, E]),
                                gtop2f[:, :, :].rearrange("p t k -> p (t k)").unsqueeze(2).to_broadcast([P, GT * 2, E]),
                                ALU.is_equal).then_inc(vec_step, 1)
                v.wait_ge(vec_step, done.up())
                tiles = slice(g * GT, (g + 1) * GT)
                v.tensor_tensor(picks[:, tiles, :], onehot[:, :, 0, :], onehot[:, :, 1, :], ALU.add).then_inc(vec_step, 1)
                v.wait_ge(vec_step, done.up())
                e2, gate = gediff[:, g % 2, :], tg[:, 1:2]

                def add_picks(t):
                    n = g * GT + t
                    v.tensor_tensor(earlier[:, n + 1, :], earlier[:, n, :], picks[:, n, :], ALU.add).then_inc(
                        picks_ready if t == GT - 1 else vec_step, 1)

                add_picks(0)
                v.wait_ge(gexp_ready, g + 1)
                v.tensor_scalar(gden[:, :], e2, 1.0, None, ALU.add).then_inc(vec_step, 1)
                v.wait_ge(vec_step, done.up(2))
                add_picks(1)
                v.reciprocal(gden[:, :], gden[:, :]).then_inc(vec_step, 1)
                v.wait_ge(vec_step, done.up(2))
                add_picks(2)
                v.tensor_scalar(gpair[:, :, 0], gden[:, :], gate, None, ALU.mult).then_inc(vec_step, 1)
                v.scalar_tensor_tensor(out=gpair[:, :, 1], in0=gden[:, :], scalar=gate, in1=e2,
                                       op0=ALU.mult, op1=ALU.mult).then_inc(vec_step, 1)
                v.wait_ge(vec_step, done.up(3))
                add_picks(3)
                v.tensor_tensor(oh_tmp[:, :, :, :].rearrange("p t k e -> p (t k) e"),
                                onehot[:, :, :, :].rearrange("p t k e -> p (t k) e"),
                                gpair[:, :, :].rearrange("p t k -> p (t k)").unsqueeze(2).to_broadcast([P, GT * 2, E]),
                                ALU.mult).then_inc(vec_step, 1)
                v.wait_ge(vec_step, done.up())
                v.wait_ge(picks_ready, g + 1)
                v.tensor_tensor(comb[:, g % 2, :, :], oh_tmp[:, :, 0, :], oh_tmp[:, :, 1, :], ALU.add).then_inc(vec_step, 1)
                v.wait_ge(vec_step, done.up())
                v.tensor_tensor(comb[:, g % 2, :, :], comb[:, g % 2, :, :],
                                alpha_bc[:, :].unsqueeze(1).to_broadcast([P, GT, E]), ALU.mult).then_inc(comb_ready, 1)
                v.wait_ge(comb_ready, g + 1)
                if g >= 2:
                    v.wait_ge(combT_ps, g - 1)
                parts = comb_split[:, g % 2, :, :, :]
                v.tensor_copy(parts[:, :, 0:2, 0:E],
                              comb[:, g % 2, :, :].unsqueeze(2).to_broadcast([P, GT, 2, E])).then_inc(vec_step, 1)
                v.wait_ge(vec_step, done.up())
                v.tensor_tensor(parts[:, :, 2, 0:E], comb[:, g % 2, :, :], parts[:, :, 0, 0:E],
                                ALU.subtract).then_inc(comb_split_ready, 1)

            def slots(g):
                v.wait_ge(rank_ps, g + 1)
                v.tensor_tensor(oh_tmp[:, :, :, :], onehot[:, :, :, :],
                                bank[7][:, 0:GT * E].rearrange("p (t e) -> p t e", t=GT).unsqueeze(2).to_broadcast(
                                    [P, GT, 2, E]), ALU.mult).then_inc(rank_read, 1)
                v.wait_ge(rank_read, g + 1)
                v.tensor_reduce(slot_f[:, :, :].rearrange("p t k -> p (t k)"),
                                oh_tmp[:, :, :, :].rearrange("p t k e -> p (t k) e"), AX.X, ALU.add).then_inc(vec_step, 1)
                v.wait_ge(vec_step, done.up())
                v.wait_ge(comb_ready, g + 1)
                if g >= 2:
                    v.wait_ge(scattered[g % 2], 16 * 2 * GT)
                v.tensor_scalar(rows[:, g % 2, :, W_COMB:W_TOK].bitcast(F32), comb[:, g % 2, :, :],
                                1.0 / (H_SCALE * W_SCALE), None, ALU.mult)
                v.tensor_copy(slot_i[:, g, :, :], slot_f[:, :, :]).then_inc(slots_ready, 1)

            def start_output(g):
                for j in range(2):
                    v.wait_ge(b2_ps, 2 * g + j + 1)
                    v.wait_ge(xn2_done, (g + 1) * GT)
                    pair = xs[:, g * GT + 2 * j:g * GT + 2 * j + 2, :].rearrange("p t d -> p (t d)")
                    v.scalar_tensor_tensor(out=pair, in0=bank[5 + j][:, :], scalar=1.0 / W_SCALE, in1=pair,
                                           op0=ALU.mult, op1=ALU.add).then_inc(init_ready, 1)

            def weights_lo(u):
                v.wait_ge(w_hi, u + 1)
                if u == NU - 1:
                    v.wait_ge(last_row_ready, 1)
                hi, lo = unit_parts(u)
                v.scalar_tensor_tensor(out=lo, in0=stage_buf[stage_of[u]], scalar=W_SCALE, in1=hi,
                                       op0=ALU.mult, op1=ALU.subtract).then_inc(w_lo, 1)

            def rows_lo(g):
                v.wait_ge(hi_ready, g + 1)
                v.tensor_tensor(rows[:, g % 2, :, P:2 * P].bitcast(F16), xn2_of[g][:, :, :],
                                rows[:, g % 2, :, 0:P].bitcast(F16), ALU.subtract).then_inc(last_row_ready, 1)

            def split_constants():
                v.wait_ge(ctx_hi_ready, 1)
                v.scalar_tensor_tensor(out=ctx_lo, in0=ctx_buf[0:NS, :, :].rearrange("p b d -> p (b d)"), scalar=C_SCALE,
                                       in1=ctx_hi[0:NS, :], op0=ALU.mult, op1=ALU.subtract).then_inc(ctx_ready, 1)
                v.wait_ge(b2_hi_ready, 1)
                r = slice(Q, Q + E)
                v.scalar_tensor_tensor(out=b2_split[r, :], in0=b2_sb[r, :], scalar=W_SCALE, in1=b2_split[r, :],
                                       op0=ALU.mult, op1=ALU.subtract).then_inc(b2_ready, 1)

            def table():
                v.wait_ge(count_ps, 1)
                v.tensor_tensor(cnt[:, :], bank[7][:, GT * E:(GT + 1) * E], region[:, :], ALU.subtract).then_inc(vec_step, 1)
                v.tensor_copy(pad_at[:, :], bank[7][0:1, GT * E:(GT + 1) * E]).then_inc(pads_ready, 1)
                v.wait_ge(vec_step, done.up())
                v.tensor_scalar(cnt_i[:, :], cnt[:, :], float(P - 1), None, ALU.add).then_inc(vec_step, 1)
                v.wait_ge(vec_step, done.up())
                v.tensor_single_scalar(tl_i[:, :], cnt_i[:, :], 7, op=ALU.logical_shift_right).then_inc(vec_step, 1)
                v.wait_ge(vec_step, done.up())
                v.tensor_scalar(tl[:, :], tl_i[:, :], 1.0, None, ALU.max).then_inc(vec_step, 1)
                v.wait_ge(vec_step, done.up())
                v.tensor_tensor_scan(ctl[:, :], ones[:, 0:E], tl[:, :], 0.0, ALU.mult, ALU.add).then_inc(vec_step, 1)
                v.wait_ge(vec_step, done.up())
                v.tensor_tensor(over[:, :, :], ctl[0:1, :].unsqueeze(1).to_broadcast([1, TILES, E]),
                                iota_t[:, :].unsqueeze(2).to_broadcast([1, TILES, E]), ALU.is_le).then_inc(vec_step, 1)
                v.wait_ge(vec_step, done.up())
                v.tensor_tensor(over2[:, :, :], over[:, :, :], tl[0:1, :].unsqueeze(1).to_broadcast([1, TILES, E]),
                                ALU.mult).then_inc(vec_step, 1)
                v.tensor_reduce(te_f[:, :], over[:, :, :], AX.X, ALU.add).then_inc(vec_step, 1)
                v.wait_ge(vec_step, done.up(2))
                v.tensor_reduce(tc_f[:, :], over2[:, :, :], AX.X, ALU.add).then_inc(vec_step, 1)
                v.tensor_scalar(te_i[:, :], te_f[:, :], float(E - 1), None, ALU.min).then_inc(vec_step, 1)
                v.wait_ge(vec_step, done.up(2))
                v.tensor_tensor(tc_f[:, :], iota_t[:, :], tc_f[:, :], ALU.subtract).then_inc(vec_step, 1)
                v.wait_ge(vec_step, done.up())
                v.tensor_scalar(tc_f[:, :], tc_f[:, :], float(P), None, ALU.mult).then_inc(vec_step, 1)
                v.wait_ge(vec_step, done.up())
                v.scalar_tensor_tensor(out=tr_i[:, :], in0=te_f[:, :], scalar=float(CAP), in1=tc_f[:, :],
                                       op0=ALU.mult, op1=ALU.add).then_inc(table_ready, 1)

            for s in range(STEPS):
                if s < NG:
                    pick_sets(s)
                    set_weights(s)
                if s == 0:
                    split_constants()
                if 0 <= s - 1 < NG:
                    add_attention(s - 1)
                if s + 2 < NG:
                    norm1_stats(s + 2)
                for u in range(lo_at[s], lo_at[s] + LO_FIRST[s]):
                    weights_lo(u)
                if 0 <= s - 2 < NG:
                    route(s - 2)
                if s - 2 == NG - 1:
                    rows_lo(NG - 1)
                if 0 <= s - 3 and s < NG + 1:
                    start_output(s - 3)
                if 0 <= s - 2 < NG:
                    slots(s - 2)
                if s == NG + 1:
                    table()
                if s >= NG + 1:
                    start_output(s - 3)
                for u in range(lo_at[s] + LO_FIRST[s], lo_at[s + 1]):
                    weights_lo(u)

            def expert_of(i):
                return v.value_load(te_i[0:1, bass.ds(i, 1)], min_val=0, max_val=E - 1)

            def fetch(i, s, e):
                v.wait_ge(xT_ps, i + 1)
                if not (isinstance(i, int) and i < 2):
                    v.wait_ge(fc1_ps, i * 2 - 2)
                v.tensor_copy(xT[:, s % 2, :, :, :].rearrange("p a k q -> p (a k q)"),
                              bank[6 + s % 2][:, 0:D].bitcast(F16)).then_inc(xT_sb, 1)
                if not (isinstance(i, int) and i < NX):
                    v.wait_ge(gelu_done, i * 2 + (2 - 2 * NX))
                v.tensor_copy(b1cur[:, s % NX, :], b1T[:, bass.ds(e, 1), :].rearrange("p a f -> p (a f)")).then_inc(b1_ready, 1)

            def keep(i, s, e):
                if not (isinstance(i, int) and i < NX):
                    v.wait_ge(added, i * 16 + (16 - 16 * NX))
                v.tensor_copy(wcur[:, s % NX:s % NX + 1], xg[:, s % NX, bass.ds(e + W_COMB, 1)].bitcast(F32))
                v.tensor_copy(tokcur[:, s % NX:s % NX + 1], xg[:, s % NX, W_TOK:ROW].bitcast(U32)).then_inc(cur_ready, 1)

            def split(i, s, half):
                c = slice(half * (F // 2), (half + 1) * (F // 2))
                v.wait_ge(gelu_done, i * 2 + (half + 1))
                if not (isinstance(i, int) and i < 2):
                    v.wait_ge(y_ps, i - 1)
                v.tensor_scalar(hhi[s % 2][:, c], h32[s % 2][:, c], H_SCALE, None, ALU.mult).then_inc(hi_done, 1)
                v.wait_ge(hi_done, i * 2 + (half + 1))
                v.scalar_tensor_tensor(out=hlo[s % 2][:, c], in0=h32[s % 2][:, c], scalar=H_SCALE,
                                       in1=hhi[s % 2][:, c], op0=ALU.mult, op1=ALU.subtract).then_inc(lo_done, 1)

            def tile(i, s, e, e1, nxt=True, first=False, units=()):
                if nxt:
                    fetch(i + 1, s + 1, e)
                for u in units:
                    weights_lo(u)
                if not first:
                    keep(i - 1, s + NX - 1, e1)
                split(i, s, 0)
                split(i, s, 1)

            v.wait_ge(table_ready, 1)
            e0 = expert_of(0)
            fetch(0, 0, e0)
            for u in range(lo_at[-1], unit_at[-1]):
                weights_lo(u)
            es = [e0]
            for i in range(HEAD):
                es.append(expert_of(i + 1))
                tile(i, i % NX, es[i + 1], es[i - 1], first=(i == 0),
                     units=range(late_at[i - 1], late_at[i]) if i else ())
            with v.Fori(0, LOOPS) as m:
                es = [expert_of(m * UNROLL + (HEAD - 1)), expert_of(m * UNROLL + HEAD)]
                for s in range(UNROLL):
                    es.append(expert_of(m * UNROLL + (HEAD + s + 1)))
                    tile(m * UNROLL + (HEAD + s), s % NX, es[s + 2], es[s])
            for i in range(HEAD + LOOPS * UNROLL, TILES):
                nxt = i < TILES - 1
                tile(i, i % NX, expert_of(i + 1) if nxt else None, expert_of(i - 1), nxt=nxt)
            keep(TILES - 1, (TILES - 1) % NX, expert_of(TILES - 1))

        @block.gpsimd
        def _(pool):
            step = Count()
            pool.memset(ident[:, :], 1.0).then_inc(pool_step, 1)
            pool.memset(before[:, :], 1.0).then_inc(pool_step, 1)
            pool.memset(pad_row[:, :], 0).then_inc(pool_step, 1)
            pool.memset(neg_half[:, :], -0.5).then_inc(pool_step, 1)
            pool.wait_ge(pool_step, step.up(4))
            pool.affine_select(out=ident[:, :], in_=ident[:, :], pattern=[[-1, P]], base=0, channel_multiplier=1,
                               compare_op=ALU.is_equal, fill=0.0).then_inc(pool_const, 1)
            pool.affine_select(out=before[:, :], in_=before[:, :], pattern=[[1, P]], base=0, channel_multiplier=-1,
                               compare_op=ALU.is_gt, fill=0.0).then_inc(pool_step, 1)
            step.up()
            pool.iota(iota_i[:, :], pattern=[[1, NS]], base=0, channel_multiplier=0)
            pool.iota(iota_ti[:, :], pattern=[[1, TILES]], base=0, channel_multiplier=0).then_inc(pool_const, 1)
            pool.iota(pad_row[:, W_TOK:ROW], pattern=[[0, 1]], base=T, channel_multiplier=1).then_inc(pool_const, 1)

            def rstd_shift(mv, rstd, shift, g, scale, stats_done, ln_done):
                r = slice(g * GT, (g + 1) * GT)
                pool.wait_ge(stats_done, (g + 1) * GT)
                pool.tensor_scalar(rstd[:, r], mv[:, r, 1], EPS, scale ** -2, ALU.add, ALU.mult).then_inc(pool_step, 1)
                pool.tensor_scalar(shift[:, r], mv[:, r, 0], -1.0, None, ALU.mult).then_inc(pool_step, 1)
                pool.wait_ge(pool_step, step.up(2))
                pool.tensor_tensor(rstd[:, r], rstd[:, r], neg_half[:, :], ALU.pow).then_inc(pool_step, 1)
                pool.wait_ge(pool_step, step.up())
                pool.tensor_tensor(shift[:, r], shift[:, r], rstd[:, r], ALU.mult).then_inc(ln_done, 1)

            def row_tokens(g):
                return pool.iota(rows[:, g % 2, :, W_TOK:ROW].rearrange("p t a -> p (t a)"), pattern=[[P, GT]],
                                 base=g * GT * P, channel_multiplier=1)

            def rows_lo(g):
                if g >= 2:
                    pool.wait_ge(scattered[g % 2], 16 * 2 * GT)
                pool.wait_ge(hi_ready, g + 1)
                row_tokens(g)
                pool.tensor_tensor(rows[:, g % 2, :, P:2 * P].bitcast(F16), xn2_of[g][:, :, :],
                                   rows[:, g % 2, :, 0:P].bitcast(F16), ALU.subtract).then_inc(row_ready, 1)

            def scatter(g, tiles):
                pool.wait_ge(slots_ready, g + 1)
                if g < NG - 1:
                    pool.wait_ge(row_ready, g + 1)
                else:
                    pool.wait_ge(last_row_ready, 1)
                for t in tiles:
                    for k in range(2):
                        pool.indirect_dma_start(
                            out=xsort[:, :], out_offset=bass.IndirectOffsetOnAxis(ap=slot_i[:, g, t, k:k + 1], axis=0),
                            in_=rows[:, g % 2, t, :], in_offset=None).then_inc(scattered[g % 2], 16)

            rstd_shift(mv1, rstd1, shift1, 0, 1.0, stats1, ln1)
            rstd_shift(mv1, rstd1, shift1, 1, 1.0, stats1, ln1)
            for s in range(STEPS):
                if 0 <= s - 1 < NG:
                    rstd_shift(mv2, rstd2, shift2, s - 1, X_SCALE, stats2, ln2)
                if s + 2 < NG:
                    rstd_shift(mv1, rstd1, shift1, s + 2, 1.0, stats1, ln1)
                if 0 <= s - 3 < NG:
                    scatter(s - 3, range(GT // 2, GT))
                if 0 <= s - 2 < NG - 1:
                    rows_lo(s - 2)
                if s - 2 == NG - 1:
                    pool.wait_ge(scattered[(NG - 1) % 2], 16 * 2 * GT)
                    row_tokens(NG - 1).then_inc(tokens_ready, 1)
                    pool.wait_ge(tokens_ready, 1)
                if 0 <= s - 2 < NG:
                    scatter(s - 2, range(GT // 2))

            def add_tile(i, s):
                pool.wait_ge(y_ready, i + 1)
                if not (isinstance(i, int) and i == 0):
                    pool.wait_ge(added, i * 16)
                pool.sem_inc(add_started, 1)
                pool.indirect_dma_start(
                    out=out[:, :], out_offset=bass.IndirectOffsetOnAxis(ap=tokcur[:, s:s + 1], axis=0),
                    in_=y_sb[:, s % 2, :], in_offset=None, compute_op=ALU.add).then_inc(added, 16)

            pool.wait_ge(out_init, 16 * NG)
            pool.wait_ge(pad_out_init, 16)
            for i in range(NX):
                add_tile(i, i)
            with pool.Fori(1, TILES // NX) as m:
                for s in range(NX):
                    add_tile(m * NX + s, s)
            for i in range(TILES // NX * NX, TILES):
                add_tile(i, i % NX)
            pool.wait_ge(added, TILES * 16)


_INS = ['x', 'ctx_2048', 'itok_Sx4_0_63', 'g_xattn', 'g_ffn', 'L0_xattn_desc_router', 'L0_xattn_W_q',
        'L0_xattn_b_q', 'L0_ffn_gate_w', 'L0_ffn_gate_b', 'L0_ffn_fc1_w', 'L0_ffn_fc1_b', 'L0_ffn_fc2_w',
        'L0_ffn_fc2_b', 'L0_ffn_alpha']


def kernel(**inputs):
    import numpy as _np
    import concourse.bacc as _bacc
    from concourse import mybir as _mybir
    from concourse.bass_utils import run_bass_kernel_spmd as _run

    nc = _bacc.Bacc("TRN2", target_bir_lowering=False, num_devices=1)
    arrays, args = {}, []
    for name in _INS:
        a = _np.ascontiguousarray(inputs[name])
        arrays[f"in_{name}_dram"] = a
        args.append(nc.dram_tensor(f"in_{name}_dram", a.shape, _mybir.dt.from_np(a.dtype), kind="ExternalInput").ap())
    shape = inputs['x'].shape
    tokens = shape[0] * shape[1]
    out = nc.dram_tensor("out_dram", [tokens + 128, shape[2]], _mybir.dt.float32, kind="ExternalOutput").ap()
    flamingo_block(nc, *args, out)
    r = _run(nc, [arrays], core_ids=[0])
    return r.results[0]["out_dram"][:tokens].reshape(shape)
```
